# Optimizing a Trainium2 kernel written in Bass

```python
import numpy as np
import jax
import jax.numpy as jnp

def _softmax(x, axis=-1):
    return jax.nn.softmax(x, axis=axis)

def _gelu(x):
    return jax.nn.gelu(x, approximate=True)

def _silu(x):
    return jax.nn.silu(x)

def _sigmoid(x):
    return jax.nn.sigmoid(x)

def _layernorm(x, axis=-1, eps=1e-05):
    m = jnp.mean(x, axis=axis, keepdims=True)
    v = jnp.var(x, axis=axis, keepdims=True)
    return (x - m) / jnp.sqrt(v + eps)

def _scatter_add(tgt, idx, src, axis=0):
    return tgt.at[idx].add(src)

def _segment_sum(src, seg, n):
    return jax.ops.segment_sum(src, seg, n)
kernel_name = 'mk_perceiver_d2_seqx_r8_2a135c'

def setup_inputs(seed: int=0):
    np.random.seed(seed)
    _w = jnp.asarray

    def _rec_inputs():
        import jax
        import jax.numpy as jnp
        _rk = jax.random.key(seed)
        x = -0.0002928 + 1 * jax.random.normal(jax.random.fold_in(_rk, 1), (32, 64, 128), jnp.float32)
        _lenS = 64 - jax.random.randint(jax.random.fold_in(_rk, 7), (32,), 0, max(1, 64 // 4) + 1, jnp.int32)
        _lenS2 = 1601 - jax.random.randint(jax.random.fold_in(_rk, 8), (32,), 0, max(1, 1601 // 4) + 1, jnp.int32)
        _ctx_1024P = jax.random.normal(jax.random.fold_in(_rk, 11), (32, 16, 128), jnp.float32)
        _ctx_1024c = jax.random.dirichlet(jax.random.fold_in(_rk, 511), 0.3 * jnp.ones((16,), jnp.float32), (32, 1601))
        _ctx_1024t = jnp.einsum('bsk,bkd->bsd', _ctx_1024c, _ctx_1024P)
        _ctx_1024t = _ctx_1024t * jax.lax.rsqrt(jnp.mean(jnp.square(_ctx_1024t)) + 1e-12) * 0.953939
        ctx_1024 = -1.39393e-06 + 0.999914 * (_ctx_1024t + 0.3 * jax.random.normal(jax.random.fold_in(_rk, 611), (32, 1601, 128), jnp.float32))
        return (x, ctx_1024)
    x, ctx_1024 = _rec_inputs()

    def _L0_xattn_setup():
        import jax, jax.numpy as jnp
        import numpy as np
        B, S, D, H = (2, 256, 128, 16)
        HD = D // H
        SCALE = HD ** (-0.5)
        NEG = -1000000000.0
        key = jax.random.key(seed)
        ks = jax.random.split(key, 7)
        w_std = 1.0 / np.sqrt(D)
        return {'query': jax.random.normal(ks[0], (B, S, D), dtype=jnp.float32), 'key': jax.random.normal(ks[1], (B, S, D), dtype=jnp.float32), 'value': jax.random.normal(ks[2], (B, S, D), dtype=jnp.float32), 'Wq': jax.random.normal(ks[3], (D, D), dtype=jnp.float32) * w_std, 'Wk': jax.random.normal(ks[4], (D, D), dtype=jnp.float32) * w_std, 'Wv': jax.random.normal(ks[5], (D, D), dtype=jnp.float32) * w_std, 'Wo': jax.random.normal(ks[6], (D, D), dtype=jnp.float32) * w_std}
    _L0_xattn_all = _L0_xattn_setup()
    _L0_xattn_in = {k: v for k, v in _L0_xattn_all.items() if k in ('Wq', 'Wk', 'Wv', 'Wo')}
    del _L0_xattn_all

    def _L0_attn_setup():
        import jax, jax.numpy as jnp
        import numpy as np
        D_MODEL, D_STATE, D_CONV, EXPAND = (128, 16, 4, 2)
        D_INNER = EXPAND * D_MODEL
        B, L = (2, 512)
        LN_EPS = 1e-05

        def _layernorm(x, gamma, beta):
            mu = jnp.mean(x, axis=-1, keepdims=True)
            var = jnp.mean(jnp.square(x - mu), axis=-1, keepdims=True)
            return (x - mu) * jax.lax.rsqrt(var + LN_EPS) * gamma + beta

        def _causal_depthwise_conv(xp, conv_w, conv_b):
            lhs = jnp.pad(xp.transpose(0, 2, 1), ((0, 0), (0, 0), (D_CONV - 1, 0)))
            out = jax.lax.conv_general_dilated(lhs, conv_w, window_strides=(1,), padding='VALID', dimension_numbers=('NCH', 'OIH', 'NCH'), feature_group_count=D_INNER)
            return out.transpose(0, 2, 1) + conv_b
        key = jax.random.key(seed)
        ks = jax.random.split(key, 6)
        x = jax.random.normal(ks[0], (B, L, D_MODEL), dtype=jnp.float32)
        ln_gamma = jnp.ones((D_MODEL,), jnp.float32)
        ln_beta = jnp.zeros((D_MODEL,), jnp.float32)
        W_in = jax.random.normal(ks[1], (2 * D_INNER, D_MODEL), jnp.float32) / np.sqrt(D_MODEL).astype(np.float32)
        conv_w = jax.random.normal(ks[2], (D_INNER, 1, D_CONV), jnp.float32) * 0.1
        conv_b = jnp.zeros((D_INNER,), jnp.float32)
        W_out = jax.random.normal(ks[3], (D_MODEL, D_INNER), jnp.float32) / np.sqrt(D_INNER).astype(np.float32)
        A = jnp.eye(D_STATE, dtype=jnp.float32)
        Bm = jax.random.normal(ks[4], (D_STATE, D_INNER), jnp.float32) * 0.01
        Cm = jax.random.normal(ks[5], (D_STATE, D_INNER), jnp.float32) * 0.01
        return dict(x=x, ln_gamma=ln_gamma, ln_beta=ln_beta, W_in=W_in, conv_w=conv_w, conv_b=conv_b, W_out=W_out, A=A, Bm=Bm, Cm=Cm)
    _L0_attn_all = _L0_attn_setup()
    _L0_attn_in = {k: v for k, v in _L0_attn_all.items() if k in ('ln_gamma', 'ln_beta', 'W_in', 'conv_w', 'conv_b', 'W_out', 'A', 'Bm', 'Cm')}
    del _L0_attn_all

    def _L0_ffn_setup():
        import jax, jax.numpy as jnp
        import numpy as np
        S, B, H = (256, 1, 128)
        N_HEADS = 16
        HEAD_DIM = H // N_HEADS
        E, K, F = (8, 2, 256)
        EPS = 1e-05

        def layernorm(x, w, b):
            mu = jnp.mean(x, axis=-1, keepdims=True)
            var = jnp.mean(jnp.square(x - mu), axis=-1, keepdims=True)
            return (x - mu) * jax.lax.rsqrt(var + EPS) * w + b
        key = jax.random.key(seed)
        ks = jax.random.split(key, 8)
        std = 0.02
        return {'x': jax.random.normal(ks[0], (S, B, H), dtype=jnp.float32), 'ln1_w': jnp.ones((H,), jnp.float32), 'ln1_b': jnp.zeros((H,), jnp.float32), 'in_proj_w': jax.random.normal(ks[1], (3 * H, H), jnp.float32) * std, 'in_proj_b': jnp.zeros((3 * H,), jnp.float32), 'out_proj_w': jax.random.normal(ks[2], (H, H), jnp.float32) * std, 'out_proj_b': jnp.zeros((H,), jnp.float32), 'ln2_w': jnp.ones((H,), jnp.float32), 'ln2_b': jnp.zeros((H,), jnp.float32), 'router_w': jax.random.normal(ks[3], (E, H), jnp.float32) * std, 'w1': jax.random.normal(ks[4], (E, H, F), jnp.float32) * std, 'w2': jax.random.normal(ks[5], (E, F, H), jnp.float32) * std}
    _L0_ffn_all = _L0_ffn_setup()
    _L0_ffn_in = {k: v for k, v in _L0_ffn_all.items() if k in ('ln1_w', 'ln1_b', 'in_proj_w', 'in_proj_b', 'out_proj_w', 'out_proj_b', 'ln2_w', 'ln2_b', 'router_w', 'w1', 'w2')}
    del _L0_ffn_all

    def _L1_xattn_setup():
        import jax, jax.numpy as jnp
        import numpy as np
        D_MODEL = 128
        NUM_HEADS = 16
        HEAD_DIM = D_MODEL // NUM_HEADS

        def _split_heads(x):
            B, S, _ = x.shape
            return x.reshape(B, S, NUM_HEADS, HEAD_DIM).transpose(0, 2, 1, 3)
        key = jax.random.key(seed)
        ks = jax.random.split(key, 11)
        B, S = (2, 256)
        s = 1.0 / np.sqrt(D_MODEL)
        return {'q': jax.random.normal(ks[0], (B, S, D_MODEL), jnp.float32), 'k': jax.random.normal(ks[1], (B, S, D_MODEL), jnp.float32), 'v': jax.random.normal(ks[2], (B, S, D_MODEL), jnp.float32), 'Wq': jax.random.normal(ks[3], (D_MODEL, D_MODEL), jnp.float32) * s, 'bq': jnp.zeros((D_MODEL,), jnp.float32), 'Wk': jax.random.normal(ks[4], (D_MODEL, D_MODEL), jnp.float32) * s, 'bk': jnp.zeros((D_MODEL,), jnp.float32), 'Wv': jax.random.normal(ks[5], (D_MODEL, D_MODEL), jnp.float32) * s, 'bv': jnp.zeros((D_MODEL,), jnp.float32), 'Wo': jax.random.normal(ks[6], (D_MODEL, D_MODEL), jnp.float32) * s, 'bo': jnp.zeros((D_MODEL,), jnp.float32)}
    _L1_xattn_all = _L1_xattn_setup()
    _L1_xattn_in = {k: v for k, v in _L1_xattn_all.items() if k in ('Wq', 'bq', 'Wk', 'bk', 'Wv', 'bv', 'Wo', 'bo')}
    del _L1_xattn_all

    def _L1_attn_setup():
        import jax, jax.numpy as jnp
        import numpy as np
        import math
        DIM = 128
        NUM_HEADS = 16
        HEAD_DIM = DIM // NUM_HEADS
        MAX_BIAS = 8.0
        SCALE = HEAD_DIM ** (-0.5)

        def _alibi_slopes(n):

            def pow2(n):
                start = 2.0 ** (-2.0 ** (-(math.log2(n) - 3)))
                return [start * start ** i for i in range(n)]
            if math.log2(n).is_integer():
                return pow2(n)
            c = 2 ** math.floor(math.log2(n))
            return pow2(c) + _alibi_slopes(2 * c)[0::2][:n - c]

        def _rotate_half(t):
            t1, t2 = jnp.split(t, 2, axis=-1)
            return jnp.concatenate([-t2, t1], axis=-1)
        key = jax.random.key(seed)
        k1, k2, k3, k4 = jax.random.split(key, 4)
        B, N, C = (2, 256, DIM)
        x = jax.random.normal(k1, (B, N, C), dtype=jnp.float32)
        qkv_w = jax.random.normal(k2, (3 * C, C), dtype=jnp.float32) * C ** (-0.5)
        proj_w = jax.random.normal(k3, (C, C), dtype=jnp.float32) * C ** (-0.5)
        proj_b = jax.random.normal(k4, (C,), dtype=jnp.float32) * 0.01
        slopes = jnp.asarray(np.array(_alibi_slopes(NUM_HEADS), dtype=np.float32))
        return {'x': x, 'qkv_w': qkv_w, 'proj_w': proj_w, 'proj_b': proj_b, 'slopes': slopes}
    _L1_attn_all = _L1_attn_setup()
    _L1_attn_in = {k: v for k, v in _L1_attn_all.items() if k in ('qkv_w', 'proj_w', 'proj_b', 'slopes')}
    del _L1_attn_all

    def _L1_ffn_setup():
        import jax, jax.numpy as jnp
        import numpy as np
        D_MODEL = 128
        N_HEADS = 16
        HEAD_DIM = D_MODEL // N_HEADS
        KV_LATENT = 64
        N_EXPERTS = 4
        D_HIDDEN = 4 * D_MODEL
        B, T = (2, 128)

        def rmsnorm(x, w, eps=1e-06):
            return w * (x * jax.lax.rsqrt(jnp.mean(x * x, axis=-1, keepdims=True) + eps))

        def layernorm(x, g, b, eps=1e-05):
            mu = jnp.mean(x, axis=-1, keepdims=True)
            var = jnp.mean((x - mu) ** 2, axis=-1, keepdims=True)
            return (x - mu) * jax.lax.rsqrt(var + eps) * g + b

        def apply_rope(x):
            t, d = (x.shape[2], x.shape[3])
            half = d // 2
            pos = jnp.arange(t, dtype=x.dtype)[:, None]
            inv_freq = 1.0 / 10000.0 ** (jnp.arange(half, dtype=x.dtype) / half)
            ang = pos * inv_freq[None, :]
            sin, cos = (jnp.sin(ang), jnp.cos(ang))
            x1, x2 = (x[..., :half], x[..., half:])
            return jnp.concatenate([x1 * cos - x2 * sin, x1 * sin + x2 * cos], axis=-1)

        def mla_attention(x, Wq, Wdkv, Wuk, Wuv, Wo, ln_g, ln_b):
            b, t, _ = x.shape
            q = (x @ Wq.T).reshape(b, t, N_HEADS, HEAD_DIM).transpose(0, 2, 1, 3)
            latent = layernorm(x @ Wdkv.T, ln_g, ln_b)
            k = (latent @ Wuk.T).reshape(b, t, N_HEADS, HEAD_DIM).transpose(0, 2, 1, 3)
            v = (latent @ Wuv.T).reshape(b, t, N_HEADS, HEAD_DIM).transpose(0, 2, 1, 3)
            q = apply_rope(q)
            k = apply_rope(k)
            scores = jnp.einsum('bhqd,bhkd->bhqk', q, k) / np.sqrt(HEAD_DIM)
            causal = jnp.tril(jnp.ones((t, t), dtype=bool))
            scores = jnp.where(causal, scores, -jnp.inf)
            attn = jax.nn.softmax(scores, axis=-1)
            out = jnp.einsum('bhqk,bhkd->bhqd', attn, v).transpose(0, 2, 1, 3).reshape(b, t, D_MODEL)
            return out @ Wo.T

        def moe(x, gate_w, gate_b, W1, b1, W2, b2):
            logits = x @ gate_w.T + gate_b
            top = jnp.argmax(logits, axis=-1)
            onehot = jax.nn.one_hot(top, N_EXPERTS, dtype=x.dtype)
            h = jax.nn.relu(jnp.einsum('btd,ehd->bteh', x, W1) + b1)
            y = jnp.einsum('bteh,edh->bted', h, W2) + b2
            return jnp.einsum('bted,bte->btd', y, onehot)
        key = jax.random.key(seed)
        ks = jax.random.split(key, 16)
        s = lambda fan_in: 1.0 / np.sqrt(fan_in)
        return {'x': jax.random.normal(ks[0], (B, T, D_MODEL), jnp.float32), 'norm1_w': jnp.ones((D_MODEL,), jnp.float32), 'norm2_w': jnp.ones((D_MODEL,), jnp.float32), 'Wq': jax.random.normal(ks[1], (D_MODEL, D_MODEL), jnp.float32) * s(D_MODEL), 'Wdkv': jax.random.normal(ks[2], (KV_LATENT, D_MODEL), jnp.float32) * s(D_MODEL), 'Wuk': jax.random.normal(ks[3], (D_MODEL, KV_LATENT), jnp.float32) * s(KV_LATENT), 'Wuv': jax.random.normal(ks[4], (D_MODEL, KV_LATENT), jnp.float32) * s(KV_LATENT), 'Wo': jax.random.normal(ks[5], (D_MODEL, D_MODEL), jnp.float32) * s(D_MODEL), 'ln_g': jnp.ones((KV_LATENT,), jnp.float32), 'ln_b': jnp.zeros((KV_LATENT,), jnp.float32), 'gate_w': jax.random.normal(ks[6], (N_EXPERTS, D_MODEL), jnp.float32) * s(D_MODEL), 'gate_b': jnp.zeros((N_EXPERTS,), jnp.float32), 'W1': jax.random.normal(ks[7], (N_EXPERTS, D_HIDDEN, D_MODEL), jnp.float32) * s(D_MODEL), 'b1': jnp.zeros((N_EXPERTS, D_HIDDEN), jnp.float32), 'W2': jax.random.normal(ks[8], (N_EXPERTS, D_MODEL, D_HIDDEN), jnp.float32) * s(D_HIDDEN), 'b2': jnp.zeros((N_EXPERTS, D_MODEL), jnp.float32)}
    _L1_ffn_all = _L1_ffn_setup()
    _L1_ffn_in = {k: v for k, v in _L1_ffn_all.items() if k in ('norm1_w', 'norm2_w', 'Wq', 'Wdkv', 'Wuk', 'Wuv', 'Wo', 'ln_g', 'ln_b', 'gate_w', 'gate_b', 'W1', 'b1', 'W2', 'b2')}
    del _L1_ffn_all
    return {'x': x, 'ctx_1024': ctx_1024, 'L0_xattn_Wq': _L0_xattn_in['Wq'], 'L0_xattn_Wk': _L0_xattn_in['Wk'], 'L0_xattn_Wv': _L0_xattn_in['Wv'], 'L0_xattn_Wo': _L0_xattn_in['Wo'], 'L0_attn_ln_gamma': _L0_attn_in['ln_gamma'], 'L0_attn_ln_beta': _L0_attn_in['ln_beta'], 'L0_attn_W_in': _L0_attn_in['W_in'], 'L0_attn_conv_w': _L0_attn_in['conv_w'], 'L0_attn_conv_b': _L0_attn_in['conv_b'], 'L0_attn_W_out': _L0_attn_in['W_out'], 'L0_attn_A': _L0_attn_in['A'], 'L0_attn_Bm': _L0_attn_in['Bm'], 'L0_attn_Cm': _L0_attn_in['Cm'], 'L0_ffn_ln1_w': _L0_ffn_in['ln1_w'], 'L0_ffn_ln1_b': _L0_ffn_in['ln1_b'], 'L0_ffn_in_proj_w': _L0_ffn_in['in_proj_w'], 'L0_ffn_in_proj_b': _L0_ffn_in['in_proj_b'], 'L0_ffn_out_proj_w': _L0_ffn_in['out_proj_w'], 'L0_ffn_out_proj_b': _L0_ffn_in['out_proj_b'], 'L0_ffn_ln2_w': _L0_ffn_in['ln2_w'], 'L0_ffn_ln2_b': _L0_ffn_in['ln2_b'], 'L0_ffn_router_w': _L0_ffn_in['router_w'], 'L0_ffn_w1': _L0_ffn_in['w1'], 'L0_ffn_w2': _L0_ffn_in['w2'], 'L1_xattn_Wq': _L1_xattn_in['Wq'], 'L1_xattn_bq': _L1_xattn_in['bq'], 'L1_xattn_Wk': _L1_xattn_in['Wk'], 'L1_xattn_bk': _L1_xattn_in['bk'], 'L1_xattn_Wv': _L1_xattn_in['Wv'], 'L1_xattn_bv': _L1_xattn_in['bv'], 'L1_xattn_Wo': _L1_xattn_in['Wo'], 'L1_xattn_bo': _L1_xattn_in['bo'], 'L1_attn_qkv_w': _L1_attn_in['qkv_w'], 'L1_attn_proj_w': _L1_attn_in['proj_w'], 'L1_attn_proj_b': _L1_attn_in['proj_b'], 'L1_attn_slopes': _L1_attn_in['slopes'], 'L1_ffn_norm1_w': _L1_ffn_in['norm1_w'], 'L1_ffn_norm2_w': _L1_ffn_in['norm2_w'], 'L1_ffn_Wq': _L1_ffn_in['Wq'], 'L1_ffn_Wdkv': _L1_ffn_in['Wdkv'], 'L1_ffn_Wuk': _L1_ffn_in['Wuk'], 'L1_ffn_Wuv': _L1_ffn_in['Wuv'], 'L1_ffn_Wo': _L1_ffn_in['Wo'], 'L1_ffn_ln_g': _L1_ffn_in['ln_g'], 'L1_ffn_ln_b': _L1_ffn_in['ln_b'], 'L1_ffn_gate_w': _L1_ffn_in['gate_w'], 'L1_ffn_gate_b': _L1_ffn_in['gate_b'], 'L1_ffn_W1': _L1_ffn_in['W1'], 'L1_ffn_b1': _L1_ffn_in['b1'], 'L1_ffn_W2': _L1_ffn_in['W2'], 'L1_ffn_b2': _L1_ffn_in['b2']}

def reference(x, ctx_1024, L0_xattn_Wq, L0_xattn_Wk, L0_xattn_Wv, L0_xattn_Wo, L0_attn_ln_gamma, L0_attn_ln_beta, L0_attn_W_in, L0_attn_conv_w, L0_attn_conv_b, L0_attn_W_out, L0_attn_A, L0_attn_Bm, L0_attn_Cm, L0_ffn_ln1_w, L0_ffn_ln1_b, L0_ffn_in_proj_w, L0_ffn_in_proj_b, L0_ffn_out_proj_w, L0_ffn_out_proj_b, L0_ffn_ln2_w, L0_ffn_ln2_b, L0_ffn_router_w, L0_ffn_w1, L0_ffn_w2, L1_xattn_Wq, L1_xattn_bq, L1_xattn_Wk, L1_xattn_bk, L1_xattn_Wv, L1_xattn_bv, L1_xattn_Wo, L1_xattn_bo, L1_attn_qkv_w, L1_attn_proj_w, L1_attn_proj_b, L1_attn_slopes, L1_ffn_norm1_w, L1_ffn_norm2_w, L1_ffn_Wq, L1_ffn_Wdkv, L1_ffn_Wuk, L1_ffn_Wuv, L1_ffn_Wo, L1_ffn_ln_g, L1_ffn_ln_b, L1_ffn_gate_w, L1_ffn_gate_b, L1_ffn_W1, L1_ffn_b1, L1_ffn_W2, L1_ffn_b2):
    import jax
    import jax.numpy as jnp

    def _L0_xattn_ref(query, key, value, Wq, Wk, Wv, Wo):
        import jax, jax.numpy as jnp
        import numpy as np
        B, S, D, H = (2, 256, 128, 16)
        HD = D // H
        SCALE = HD ** (-0.5)
        NEG = -1000000000.0
        b, sq, d = query.shape
        sk = key.shape[1]
        q = (query @ Wq.T).reshape(b, sq, H, HD).transpose(0, 2, 1, 3)
        k = (key @ Wk.T).reshape(b, sk, H, HD).transpose(0, 2, 1, 3)
        v = (value @ Wv.T).reshape(b, sk, H, HD).transpose(0, 2, 1, 3)
        scores = jnp.einsum('bhqd,bhkd->bhqk', q, k) * SCALE
        causal = jnp.arange(sq)[:, None] >= jnp.arange(sk)[None, :]
        scores = jnp.where(causal[None, None], scores, NEG)
        attn = jax.nn.softmax(scores, axis=-1)
        out = jnp.einsum('bhqk,bhkd->bhqd', attn, v)
        out = out.transpose(0, 2, 1, 3).reshape(b, sq, d)
        return out @ Wo.T

    def _L0_attn_ref(x, ln_gamma, ln_beta, W_in, conv_w, conv_b, W_out, A, Bm, Cm):
        import jax, jax.numpy as jnp
        import numpy as np
        D_MODEL, D_STATE, D_CONV, EXPAND = (128, 16, 4, 2)
        D_INNER = EXPAND * D_MODEL
        B, L = (2, 512)
        LN_EPS = 1e-05

        def _layernorm(x, gamma, beta):
            mu = jnp.mean(x, axis=-1, keepdims=True)
            var = jnp.mean(jnp.square(x - mu), axis=-1, keepdims=True)
            return (x - mu) * jax.lax.rsqrt(var + LN_EPS) * gamma + beta

        def _causal_depthwise_conv(xp, conv_w, conv_b):
            lhs = jnp.pad(xp.transpose(0, 2, 1), ((0, 0), (0, 0), (D_CONV - 1, 0)))
            out = jax.lax.conv_general_dilated(lhs, conv_w, window_strides=(1,), padding='VALID', dimension_numbers=('NCH', 'OIH', 'NCH'), feature_group_count=D_INNER)
            return out.transpose(0, 2, 1) + conv_b
        xn = _layernorm(x, ln_gamma, ln_beta)
        xz = jnp.einsum('bld,ed->ble', xn, W_in)
        x_part, z = jnp.split(xz, 2, axis=-1)
        x_conv = jax.nn.silu(_causal_depthwise_conv(x_part, conv_w, conv_b))
        u_seq = x_part.transpose(1, 0, 2)
        xc_seq = x_conv.transpose(1, 0, 2)
        z_seq = z.transpose(1, 0, 2)

        def step(state, inp):
            u_t, xc_t, z_t = inp
            state = state @ A.T + u_t @ Bm.T
            out = (xc_t + state @ Cm) * jax.nn.sigmoid(z_t)
            return (state, out)
        state0 = jnp.zeros((x.shape[0], D_STATE), x.dtype)
        _, ys = jax.lax.scan(step, state0, (u_seq, xc_seq, z_seq))
        y = ys.transpose(1, 0, 2)
        residual = jnp.einsum('bli,di->bld', y, W_out)
        return x + residual

    def _L0_ffn_ref(x, ln1_w, ln1_b, in_proj_w, in_proj_b, out_proj_w, out_proj_b, ln2_w, ln2_b, router_w, w1, w2):
        import jax, jax.numpy as jnp
        import numpy as np
        S, B, H = (256, 1, 128)
        N_HEADS = 16
        HEAD_DIM = H // N_HEADS
        E, K, F = (8, 2, 256)
        EPS = 1e-05

        def layernorm(x, w, b):
            mu = jnp.mean(x, axis=-1, keepdims=True)
            var = jnp.mean(jnp.square(x - mu), axis=-1, keepdims=True)
            return (x - mu) * jax.lax.rsqrt(var + EPS) * w + b
        s, b, h = x.shape
        hn = layernorm(x, ln1_w, ln1_b)
        qkv = hn @ in_proj_w.T + in_proj_b
        q, k, v = jnp.split(qkv, 3, axis=-1)
        q = q.reshape(s, b, N_HEADS, HEAD_DIM)
        k = k.reshape(s, b, N_HEADS, HEAD_DIM)
        v = v.reshape(s, b, N_HEADS, HEAD_DIM)
        scores = jnp.einsum('sbnd,tbnd->bnst', q, k) / np.sqrt(HEAD_DIM)
        causal = jnp.tril(jnp.ones((s, s), bool))
        scores = jnp.where(causal[None, None], scores, -jnp.inf)
        probs = jax.nn.softmax(scores, axis=-1)
        attn = jnp.einsum('bnst,tbnd->sbnd', probs, v).reshape(s, b, h)
        attn = attn @ out_proj_w.T + out_proj_b
        x1 = x + attn
        hn2 = layernorm(x1, ln2_w, ln2_b).reshape(s * b, h)
        logits = hn2 @ router_w.T
        rp = jax.nn.softmax(logits, axis=-1)
        topw, topi = jax.lax.top_k(rp, K)
        gates = jnp.sum(jax.nn.one_hot(topi, E, dtype=hn2.dtype) * topw[..., None], axis=1)
        hmid = jax.nn.gelu(jnp.einsum('th,ehf->tef', hn2, w1), approximate=False)
        y = jnp.einsum('tef,efh->th', hmid * gates[:, :, None], w2)
        return x1 + y.reshape(s, b, h)

    def _L1_xattn_ref(q, k, v, Wq, bq, Wk, bk, Wv, bv, Wo, bo):
        import jax, jax.numpy as jnp
        import numpy as np
        D_MODEL = 128
        NUM_HEADS = 16
        HEAD_DIM = D_MODEL // NUM_HEADS

        def _split_heads(x):
            B, S, _ = x.shape
            return x.reshape(B, S, NUM_HEADS, HEAD_DIM).transpose(0, 2, 1, 3)
        B, S, _ = q.shape
        qh = _split_heads(q @ Wq.T + bq)
        kh = _split_heads(k @ Wk.T + bk)
        vh = _split_heads(v @ Wv.T + bv)
        scale = 1.0 / jnp.sqrt(jnp.asarray(HEAD_DIM, qh.dtype))
        scores = jnp.einsum('bhqd,bhkd->bhqk', qh, kh) * scale
        attn = jax.nn.softmax(scores, axis=-1)
        out = jnp.einsum('bhqk,bhkd->bhqd', attn, vh)
        out = out.transpose(0, 2, 1, 3).reshape(B, S, D_MODEL)
        return out @ Wo.T + bo

    def _L1_attn_ref(x, qkv_w, proj_w, proj_b, slopes):
        import jax, jax.numpy as jnp
        import numpy as np
        import math
        DIM = 128
        NUM_HEADS = 16
        HEAD_DIM = DIM // NUM_HEADS
        MAX_BIAS = 8.0
        SCALE = HEAD_DIM ** (-0.5)

        def _alibi_slopes(n):

            def pow2(n):
                start = 2.0 ** (-2.0 ** (-(math.log2(n) - 3)))
                return [start * start ** i for i in range(n)]
            if math.log2(n).is_integer():
                return pow2(n)
            c = 2 ** math.floor(math.log2(n))
            return pow2(c) + _alibi_slopes(2 * c)[0::2][:n - c]

        def _rotate_half(t):
            t1, t2 = jnp.split(t, 2, axis=-1)
            return jnp.concatenate([-t2, t1], axis=-1)
        B, N, C = x.shape
        H, D = (NUM_HEADS, HEAD_DIM)
        qkv = (x @ qkv_w.T).reshape(B, N, 3, H, D).transpose(2, 0, 3, 1, 4)
        q, k, v = (qkv[0], qkv[1], qkv[2])
        inv_freq = 1.0 / 10000.0 ** (jnp.arange(0, D, 2, dtype=jnp.float32) / D)
        freqs = jnp.arange(N, dtype=jnp.float32)[:, None] * inv_freq[None, :]
        sin = jnp.tile(jnp.sin(freqs), (1, 2))
        cos = jnp.tile(jnp.cos(freqs), (1, 2))
        q = q * cos + _rotate_half(q) * sin
        k = k * cos + _rotate_half(k) * sin
        attn = jnp.einsum('bhqd,bhkd->bhqk', q, k) * SCALE
        pos = jnp.arange(N, dtype=jnp.float32)
        diff = pos[None, :] - pos[:, None]
        diff = jnp.where(diff > 0, 0.0, diff)
        alibi = diff[None, :, :] * slopes[:, None, None] * MAX_BIAS
        attn = attn + alibi[None]
        w = jax.nn.softmax(attn, axis=-1)
        out = jnp.einsum('bhqk,bhkd->bhqd', w, v)
        out = out.transpose(0, 2, 1, 3).reshape(B, N, C)
        return out @ proj_w.T + proj_b

    def _L1_ffn_ref(x, norm1_w, norm2_w, Wq, Wdkv, Wuk, Wuv, Wo, ln_g, ln_b, gate_w, gate_b, W1, b1, W2, b2):
        import jax, jax.numpy as jnp
        import numpy as np
        D_MODEL = 128
        N_HEADS = 16
        HEAD_DIM = D_MODEL // N_HEADS
        KV_LATENT = 64
        N_EXPERTS = 4
        D_HIDDEN = 4 * D_MODEL
        B, T = (2, 128)

        def rmsnorm(x, w, eps=1e-06):
            return w * (x * jax.lax.rsqrt(jnp.mean(x * x, axis=-1, keepdims=True) + eps))

        def layernorm(x, g, b, eps=1e-05):
            mu = jnp.mean(x, axis=-1, keepdims=True)
            var = jnp.mean((x - mu) ** 2, axis=-1, keepdims=True)
            return (x - mu) * jax.lax.rsqrt(var + eps) * g + b

        def apply_rope(x):
            t, d = (x.shape[2], x.shape[3])
            half = d // 2
            pos = jnp.arange(t, dtype=x.dtype)[:, None]
            inv_freq = 1.0 / 10000.0 ** (jnp.arange(half, dtype=x.dtype) / half)
            ang = pos * inv_freq[None, :]
            sin, cos = (jnp.sin(ang), jnp.cos(ang))
            x1, x2 = (x[..., :half], x[..., half:])
            return jnp.concatenate([x1 * cos - x2 * sin, x1 * sin + x2 * cos], axis=-1)

        def mla_attention(x, Wq, Wdkv, Wuk, Wuv, Wo, ln_g, ln_b):
            b, t, _ = x.shape
            q = (x @ Wq.T).reshape(b, t, N_HEADS, HEAD_DIM).transpose(0, 2, 1, 3)
            latent = layernorm(x @ Wdkv.T, ln_g, ln_b)
            k = (latent @ Wuk.T).reshape(b, t, N_HEADS, HEAD_DIM).transpose(0, 2, 1, 3)
            v = (latent @ Wuv.T).reshape(b, t, N_HEADS, HEAD_DIM).transpose(0, 2, 1, 3)
            q = apply_rope(q)
            k = apply_rope(k)
            scores = jnp.einsum('bhqd,bhkd->bhqk', q, k) / np.sqrt(HEAD_DIM)
            causal = jnp.tril(jnp.ones((t, t), dtype=bool))
            scores = jnp.where(causal, scores, -jnp.inf)
            attn = jax.nn.softmax(scores, axis=-1)
            out = jnp.einsum('bhqk,bhkd->bhqd', attn, v).transpose(0, 2, 1, 3).reshape(b, t, D_MODEL)
            return out @ Wo.T

        def moe(x, gate_w, gate_b, W1, b1, W2, b2):
            logits = x @ gate_w.T + gate_b
            top = jnp.argmax(logits, axis=-1)
            onehot = jax.nn.one_hot(top, N_EXPERTS, dtype=x.dtype)
            h = jax.nn.relu(jnp.einsum('btd,ehd->bteh', x, W1) + b1)
            y = jnp.einsum('bteh,edh->bted', h, W2) + b2
            return jnp.einsum('bted,bte->btd', y, onehot)
        x = x + mla_attention(rmsnorm(x, norm1_w), Wq, Wdkv, Wuk, Wuv, Wo, ln_g, ln_b)
        x = x + moe(rmsnorm(x, norm2_w), gate_w, gate_b, W1, b1, W2, b2)
        return x
    x = x + _L0_xattn_ref(_layernorm(x, axis=-1), ctx_1024, ctx_1024, L0_xattn_Wq, L0_xattn_Wk, L0_xattn_Wv, L0_xattn_Wo)
    x = x + _L0_attn_ref(_layernorm(x, axis=-1), L0_attn_ln_gamma, L0_attn_ln_beta, L0_attn_W_in, L0_attn_conv_w, L0_attn_conv_b, L0_attn_W_out, L0_attn_A, L0_attn_Bm, L0_attn_Cm)
    x = x + _L0_ffn_ref(_layernorm(x, axis=-1), L0_ffn_ln1_w, L0_ffn_ln1_b, L0_ffn_in_proj_w, L0_ffn_in_proj_b, L0_ffn_out_proj_w, L0_ffn_out_proj_b, L0_ffn_ln2_w, L0_ffn_ln2_b, L0_ffn_router_w, L0_ffn_w1, L0_ffn_w2)
    x = x + _L1_xattn_ref(_layernorm(x, axis=-1), ctx_1024, ctx_1024, L1_xattn_Wq, L1_xattn_bq, L1_xattn_Wk, L1_xattn_bk, L1_xattn_Wv, L1_xattn_bv, L1_xattn_Wo, L1_xattn_bo)
    x = x + _L1_attn_ref(_layernorm(x, axis=-1), L1_attn_qkv_w, L1_attn_proj_w, L1_attn_proj_b, L1_attn_slopes)
    x = x + _L1_ffn_ref(_layernorm(x, axis=-1), L1_ffn_norm1_w, L1_ffn_norm2_w, L1_ffn_Wq, L1_ffn_Wdkv, L1_ffn_Wuk, L1_ffn_Wuv, L1_ffn_Wo, L1_ffn_ln_g, L1_ffn_ln_b, L1_ffn_gate_w, L1_ffn_gate_b, L1_ffn_W1, L1_ffn_b1, L1_ffn_W2, L1_ffn_b2)
    return x

_drawn_inputs = setup_inputs


def setup_inputs(seed=0):
    import zlib

    import numpy as np

    out = dict(_drawn_inputs(seed))
    spreads = {'L0_attn_ln_gamma': (1.0, 0.6),
     'L0_attn_ln_beta': (0.0, 0.692),
     'L0_attn_conv_b': (0.0, 0.268),
     'L0_ffn_ln1_w': (1.0, 0.6),
     'L0_ffn_ln1_b': (0.0, 0.8),
     'L0_ffn_in_proj_b': (0.0, 0.386),
     'L0_ffn_out_proj_b': (0.0, 0.1),
     'L0_ffn_ln2_w': (1.0, 0.6),
     'L0_ffn_ln2_b': (0.0, 0.8),
     'L1_xattn_bq': (0.0, 0.603),
     'L1_xattn_bk': (0.0, 2.0),
     'L1_xattn_bv': (0.0, 0.357),
     'L1_xattn_bo': (0.0, 0.1),
     'L1_ffn_norm1_w': (1.0, 0.2),
     'L1_ffn_norm2_w': (1.0, 0.2),
     'L1_ffn_ln_g': (1.0, 0.2),
     'L1_ffn_ln_b': (0.0, 0.1),
     'L1_ffn_gate_b': (0.0, 0.1),
     'L1_ffn_b1': (0.0, 0.52),
     'L1_ffn_b2': (0.0, 0.351)}
    factors = {'L0_ffn_in_proj_w': 4.749,
     'L0_ffn_out_proj_w': 2.668,
     'L0_ffn_router_w': 8.0,
     'L0_ffn_w1': 8.0,
     'L0_ffn_w2': 7.182,
     'L1_attn_proj_b': 23.684}
    for name, (base, spread) in spreads.items():
        noise = np.random.default_rng([zlib.crc32(name.encode()), seed]).standard_normal(out[name].shape)
        drawn = base * np.exp(spread * noise) if base else spread * noise
        out[name] = jnp.asarray(drawn.astype(out[name].dtype))
    for name, factor in factors.items():
        out[name] = (out[name] * factor).astype(out[name].dtype)
    return out
```

```python
from contextlib import ExitStack

import numpy as np

import concourse.bass as bass
from concourse import mybir

F32 = mybir.dt.float32
F32R = mybir.dt.float32r
BF16 = mybir.dt.bfloat16
U32 = mybir.dt.uint32
ALU = mybir.AluOpType
ACT = mybir.ActivationFunctionType
AX = mybir.AxisListType

P = 128
B, S, D = 32, 64, 128
T = B * S
H, HD = 16, 8
KEYS = 1601
TILES = T // P
SLOTS = 4
SCALE = float(HD) ** -0.5
NEG = -1.0e30

COLS = ["L0_attn_ln_gamma", "L0_attn_ln_beta", "L0_ffn_ln1_w", "L0_ffn_ln1_b", "L0_ffn_ln2_w", "L0_ffn_ln2_b",
        "L0_ffn_bq", "L0_ffn_bk", "L1_xattn_bq", "L1_xattn_bk", "L1_ffn_norm1_w", "L1_ffn_norm2_w",
        "L1_ffn_ln_g", "L1_ffn_ln_b", "conv_b0", "conv_b1", "L1_xattn_bv"]
ROWS = ["L0_ffn_bv", "L0_ffn_out_proj_b", "L1_xattn_bv", "L1_xattn_bo", "L1_attn_proj_b"]


def tiles_by_batch(x):
    return x.rearrange("(t p) d -> t p d", p=P)


def tiles_by_position(x):
    return x.rearrange("(b t q) d -> t q b d", b=B, q=4)


def end_phase(nc, sems):
    nc.clear_and_free_semaphores(sems)
    nc.all_engine_barrier()


def attention_phase(nc, dr, name, *, x_in, outs, L=S, by_position=False, second_norm=None, gamma=None, beta=None,
                    w=None, q_bias=None, k_bias=None, v_bias=None, o_bias=None, rope=False, ctx=None,
                    latent=None, alibi=False, keep_norm=False):
    NB = P // L
    HG = P // L
    NG = H // HG
    SC = H * L
    PIECES = P // B if by_position else 1

    with ExitStack() as st:
        def sb(n, shape, dt=F32):
            return st.enter_context(nc.sbuf_tensor(f"{name}_{n}", shape, dt))

        sems = []

        def sem(n):
            sems.append(nc.alloc_semaphore(f"{name}_{n}"))
            return sems[-1]

        WQK = 4 if rope else 2
        w_in = sb("w_in", [P, WQK + 1, P])
        w_out = sb("w_out", [P, P])
        cols = sb("cols", [P, len(COLS)])
        brow = sb("brow", [1, len(ROWS), P])
        ones = sb("ones", [1, P])
        ident = sb("ident", [P, P])
        ident_b = sb("ident_b", [P, P], BF16)
        mask = sb("mask", [P, SC], BF16)
        head_mask = sb("head_mask", [P, H])
        v_mask = sb("v_mask", [P, HG * HD])
        eps = sb("eps", [P, 4])
        bias_full = sb("bias_full", [P, SC]) if alibi else None
        dist = sb("dist", [P, L]) if alibi else None
        slopes = sb("slopes", [P, H]) if alibi else None
        table = sb("table", [P, 4, P]) if rope else None
        w_lat = sb("w_lat", [P, 64]) if latent else None
        wk_lat = sb("wk_lat", [64, WQK - 1, P]) if latent else None

        per = range(SLOTS)
        x_t = [sb(f"x{s}", [P, P]) for s in per]
        c_t = [sb(f"c{s}", [P, P]) for s in per] if ctx is not None else None
        mom = [sb(f"mom{s}", [P, 6]) for s in per]
        mv = [sb(f"mv{s}", [P, 2]) for s in per]
        rstd = [sb(f"rstd{s}", [P, 2]) for s in per]
        h = [sb(f"h{s}", [P, P]) for s in per]
        mom2 = [sb(f"mom2{s}", [P, 6]) for s in per]
        mv2 = [sb(f"mv2{s}", [P, 2]) for s in per]
        rstd2 = [sb(f"rstd2{s}", [P, 2]) for s in per]
        hn = [sb(f"hn{s}", [P, P]) for s in per] if second_norm else h
        hT = [sb(f"hT{s}", [P, P]) for s in per]
        lat = [sb(f"lat{s}", [P, 64]) for s in per] if latent else None
        latT = [sb(f"latT{s}", [64, P]) for s in per] if latent else None
        qT = [sb(f"qT{s}", [P, P]) for s in per]
        kT = [sb(f"kT{s}", [P, P]) for s in per]
        qR = [sb(f"qR{s}", [P, P]) for s in per] if rope else None
        kR = [sb(f"kR{s}", [P, P]) for s in per] if rope else None
        k_bd = [sb(f"k_bd{s}", [P, NB, H, L]) for s in per]
        v_bd = [sb(f"v_bd{s}", [P, NB, NG, HG * HD]) for s in per]
        nmax = [sb(f"nmax{s}", [P, H]) for s in per]
        probs = [sb(f"probs{s}", [P, H, L]) for s in per]
        den = [sb(f"den{s}", [P, H]) for s in per]
        rden = [sb(f"rden{s}", [P, H]) for s in per]
        probsT = [sb(f"probsT{s}", [P, NG, P]) for s in per]
        att = [sb(f"att{s}", [P, P]) for s in per]
        attT = [sb(f"attT{s}", [P, P]) for s in per]
        y_a = [sb(f"ya{s}", [P, P]) for s in per]
        y_b = [sb(f"yb{s}", [P, P]) for s in per] if keep_norm else None
        ps = [st.enter_context(nc.psum_tensor(f"{name}_ps{s}", [P, 2, 512], F32)) for s in per]

        weights_loaded = sem("weights_loaded")
        consts_ready = sem("consts_ready")
        alibi_ready = sem("alibi_ready")
        x_loaded = [sem(f"x_loaded{s}") for s in per]
        wait_carried = sem("wait_carried")
        stats_ready = sem("stats_ready")
        moments_ready = sem("moments_ready")
        eps_added = sem("eps_added")
        rstd_ready = sem("rstd_ready")
        h_ready = sem("h_ready")
        stats2_ready = sem("stats2_ready")
        moments2_ready = sem("moments2_ready")
        square_ready = sem("square_ready")
        eps2_added = sem("eps2_added")
        rstd2_ready = sem("rstd2_ready")
        hn_ready = sem("hn_ready")
        hT_in_psum = sem("hT_in_psum")
        hT_ready = sem("hT_ready")
        lat_in_psum = sem("lat_in_psum")
        lat_stats = sem("lat_stats")
        lat_moments = sem("lat_moments")
        lat_eps = sem("lat_eps")
        lat_rstd = sem("lat_rstd")
        lat_ready = sem("lat_ready")
        latT_in_psum = sem("latT_in_psum")
        latT_ready = sem("latT_ready")
        qkv_in_psum = sem("qkv_in_psum")
        qk_products = sem("qk_products")
        k_ready = sem("k_ready")
        qkv_ready = sem("qkv_ready")
        k_spread = sem("k_spread")
        scores_in_psum = sem("scores_in_psum")
        max_ready = sem("max_ready")
        shifted = sem("shifted")
        probs_ready = sem("probs_ready")
        den_ready = sem("den_ready")
        rden_ready = sem("rden_ready")
        probsT_in_psum = sem("probsT_in_psum")
        probsT_ready = sem("probsT_ready")
        att_in_psum = sem("att_in_psum")
        att_ready = sem("att_ready")
        attT_in_psum = sem("attT_in_psum")
        attT_ready = sem("attT_ready")
        out_in_psum = sem("out_in_psum")
        out_a_ready = sem("out_a_ready")
        out_ready = sem("out_ready")
        stored = [sem(f"stored{s}") for s in per]

        loads = [(w_in, dr[w][:, 0:WQK + 1, :]), (w_out, dr[w][:, WQK + 1, :]), (cols, dr["cols"]),
                 (brow, dr["rows"]), (ident, dr["ident"]), (head_mask, dr["head_mask"]),
                 (v_mask, dr[f"v_mask{L}"])]
        if latent:
            loads += [(w_lat, dr["w_lat"]), (wk_lat, dr["wk_lat"])]
        if rope:
            loads += [(table, dr["rope"])]
        if alibi:
            loads += [(dist, dr["dist"]), (slopes, dr["slopes"])]
        else:
            loads += [(mask[:].bitcast(F32), dr[f"mask{L}"])]
        xv = (tiles_by_position if by_position else tiles_by_batch)(x_in)
        ov = [tiles_by_batch(o) for o in outs]
        LOADS = PIECES + (ctx is not None)

        def col(n):
            return cols[:, COLS.index(n):COLS.index(n) + 1]

        def count(i, s):
            return i * SLOTS + (s + 1)

        with nc.Block() as block:
            @block.sync
            def _(sp):
                for dst, src in loads:
                    sp.dma_start(dst[:], src).then_inc(weights_loaded, 16)
                with sp.Fori(0, TILES // SLOTS) as i:
                    for s in per:
                        sp.wait_ge(stored[s], i * (16 * len(outs)) + 1)
                        for q in range(PIECES):
                            sp.dma_start(x_t[s][q * B:(q + 1) * B] if by_position else x_t[s][:],
                                         xv[i * SLOTS + s, q] if by_position else xv[i * SLOTS + s]).then_inc(x_loaded[s], 16)
                        if ctx is not None:
                            sp.dma_start(c_t[s][:].rearrange("p (b k) -> p b k", b=NB),
                                         ctx[:, bass.ds(i * (SLOTS * NB) + s * NB, NB), 0:L]).then_inc(x_loaded[s], 16)
                    for s in per:
                        sp.wait_ge(out_ready, count(i, s))
                        for o, buf in zip(ov, (y_a, y_b) if keep_norm else (y_a,)):
                            sp.dma_start(o[i * SLOTS + s], buf[s][:]).then_inc(stored[s], 16)
                for s in per:
                    sp.wait_ge(stored[s], 1 + 16 * len(outs) * (TILES // SLOTS))

            @block.gpsimd
            def _(pool):
                for s in per:
                    pool.sem_inc(stored[s], 1)
                nc.gpsimd.memset(ones[:], 1.0).then_inc(consts_ready, 1)
                nc.gpsimd.memset(eps[:, 0:1], -0.5).then_inc(consts_ready, 1)
                nc.gpsimd.memset(eps[:, 1:2], 1e-5).then_inc(consts_ready, 1)
                nc.gpsimd.memset(eps[:, 2:3], 1e-6).then_inc(consts_ready, 1)
                pool.wait_ge(weights_loaded, 16 * len(loads))
                nc.gpsimd.tensor_copy(ident_b[:], ident[:]).then_inc(consts_ready, 1)
                pool.wait_ge(consts_ready, 5)
                with pool.Fori(0, TILES // SLOTS) as i:
                    for s in per:
                        pool.wait_ge(moments_ready, count(i, s))
                        nc.gpsimd.tensor_tensor(rstd[s][:, 0:1], mv[s][:, 1:2], eps[:, 1:2], ALU.add).then_inc(eps_added, 1)
                        pool.wait_ge(eps_added, count(i, s))
                        nc.gpsimd.tensor_tensor(rstd[s][:, 1:2], rstd[s][:, 0:1], eps[:, 0:1], ALU.pow).then_inc(rstd_ready, 1)
                    if second_norm:
                        e = 2 if second_norm == "rms" else 1
                        for s in per:
                            pool.wait_ge(square_ready if second_norm == "rms" else moments2_ready, count(i, s))
                            nc.gpsimd.tensor_tensor(rstd2[s][:, 0:1], mv2[s][:, 1:2], eps[:, e:e + 1], ALU.add).then_inc(eps2_added, 1)
                            pool.wait_ge(eps2_added, count(i, s))
                            nc.gpsimd.tensor_tensor(rstd2[s][:, 1:2], rstd2[s][:, 0:1], eps[:, 0:1], ALU.pow).then_inc(rstd2_ready, 1)
                    if latent:
                        for s in per:
                            pool.wait_ge(lat_moments, count(i, s))
                            nc.gpsimd.tensor_tensor(rstd[s][:, 0:1], mv[s][:, 1:2], eps[:, 1:2], ALU.add).then_inc(lat_eps, 1)
                            pool.wait_ge(lat_eps, count(i, s))
                            nc.gpsimd.tensor_tensor(rstd[s][:, 1:2], rstd[s][:, 0:1], eps[:, 0:1], ALU.pow).then_inc(lat_rstd, 1)
                    for s in per:
                        pool.wait_ge(k_ready, count(i, s))
                        for b in range(NB):
                            m = nc.gpsimd.tensor_tensor(
                                k_bd[s][:, b], kT[s][:, b * L:(b + 1) * L].unsqueeze(1).broadcast_to([P, H, L]),
                                head_mask[:].unsqueeze(2).broadcast_to([P, H, L]), ALU.mult)
                        m.then_inc(k_spread, 1)

            @block.scalar
            def _(act):
                act.wait_ge(weights_loaded, 16 * len(loads))
                with act.Fori(0, TILES // SLOTS) as i:
                    for s in per:
                        act.wait_ge(hT_in_psum, count(i, s))
                        if gamma:
                            nc.scalar.activation(hT[s][:], ps[s][:, 0, 0:P], ACT.Identity, scale=col(gamma),
                                                 bias=col(beta) if beta else 0.0).then_inc(hT_ready, 1)
                        else:
                            nc.scalar.activation(hT[s][:], ps[s][:, 0, 0:P], ACT.Copy).then_inc(hT_ready, 1)
                    if latent:
                        for s in per:
                            act.wait_ge(latT_in_psum, count(i, s))
                            nc.scalar.activation(latT[s][:], ps[s][0:64, 1, P:2 * P], ACT.Identity,
                                                 scale=col("L1_ffn_ln_g")[0:64], bias=col("L1_ffn_ln_b")[0:64]).then_inc(latT_ready, 1)
                    for s in per:
                        act.wait_ge(shifted, count(i, s))
                        nc.scalar.activation(probs[s][:], probs[s][:], ACT.Exp).then_inc(probs_ready, 1)
                    for s in per:
                        act.wait_ge(probsT_in_psum, count(i, s))
                        nc.scalar.activation(probsT[s][:].rearrange("p g n -> p (g n)"),
                                             ps[s][:].rearrange("p a n -> p (a n)")[:, 0:NG * P], ACT.Copy).then_inc(probsT_ready, 1)
                    for s in per:
                        act.wait_ge(attT_in_psum, count(i, s))
                        nc.scalar.activation(attT[s][:], ps[s][:, 1, 0:P], ACT.Copy).then_inc(attT_ready, 1)

            @block.vector
            def _(dve):
                dve.wait_ge(weights_loaded, 16 * len(loads))
                if alibi:
                    nc.vector.tensor_tensor(bias_full[:].rearrange("p (h k) -> p h k", h=H),
                                            dist[:].unsqueeze(1).broadcast_to([P, H, L]),
                                            slopes[:].unsqueeze(2).broadcast_to([P, H, L]), ALU.mult).then_inc(alibi_ready, 1)
                with dve.Fori(0, TILES // SLOTS) as i:
                    for s in per:
                        dve.wait_ge(x_loaded[s], i * (16 * LOADS) + 16 * LOADS)
                        nc.vector.bn_stats(mom[s][:], x_t[s][:]).then_inc(stats_ready, 1)
                    for s in per:
                        dve.wait_ge(stats_ready, count(i, s))
                        dve.sem_inc(wait_carried, 1)
                        nc.vector.bn_aggr(mv[s][:], mom[s][:]).then_inc(moments_ready, 1)
                    for s in per:
                        dve.wait_ge(rstd_ready, count(i, s))
                        nc.vector.tensor_scalar(h[s][:], x_t[s][:], mv[s][:, 0:1], rstd[s][:, 1:2],
                                                ALU.subtract, ALU.mult).then_inc(h_ready, 1)
                    if second_norm:
                        for s in per:
                            dve.wait_ge(h_ready, count(i, s))
                            nc.vector.bn_stats(mom2[s][:], h[s][:]).then_inc(stats2_ready, 1)
                        for s in per:
                            dve.wait_ge(stats2_ready, count(i, s))
                            dve.sem_inc(wait_carried, 1)
                            nc.vector.bn_aggr(mv2[s][:], mom2[s][:]).then_inc(moments2_ready, 1)
                        if second_norm == "rms":
                            for s in per:
                                dve.wait_ge(moments2_ready, count(i, s))
                                nc.vector.scalar_tensor_tensor(mv2[s][:, 1:2], mv2[s][:, 0:1], mv2[s][:, 0:1], mv2[s][:, 1:2],
                                                               ALU.mult, ALU.add).then_inc(square_ready, 1)
                        for s in per:
                            dve.wait_ge(rstd2_ready, count(i, s))
                            if second_norm == "rms":
                                nc.vector.tensor_scalar(hn[s][:], h[s][:], rstd2[s][:, 1:2], None, ALU.mult).then_inc(hn_ready, 1)
                            else:
                                nc.vector.tensor_scalar(hn[s][:], h[s][:], mv2[s][:, 0:1], rstd2[s][:, 1:2],
                                                        ALU.subtract, ALU.mult).then_inc(hn_ready, 1)
                    if latent:
                        for s in per:
                            dve.wait_ge(lat_in_psum, count(i, s))
                            nc.vector.bn_stats(mom[s][:], ps[s][:, 1, 0:64]).then_inc(lat_stats, 1)
                        for s in per:
                            dve.wait_ge(lat_stats, count(i, s))
                            dve.sem_inc(wait_carried, 1)
                            nc.vector.bn_aggr(mv[s][:], mom[s][:]).then_inc(lat_moments, 1)
                        for s in per:
                            dve.wait_ge(lat_rstd, count(i, s))
                            nc.vector.tensor_scalar(lat[s][:], ps[s][:, 1, 0:64], mv[s][:, 0:1], rstd[s][:, 1:2],
                                                    ALU.subtract, ALU.mult).then_inc(lat_ready, 1)
                    for s in per:
                        dve.wait_ge(qkv_in_psum, count(i, s))
                        q_ps, k_ps = ps[s][:, 0, 0:P], ps[s][:, 0, P:2 * P]
                        if rope:
                            nc.vector.tensor_tensor(kT[s][:], k_ps, table[:, 2], ALU.mult)
                            nc.vector.tensor_tensor(kR[s][:], ps[s][:, 0, 3 * P:4 * P], table[:, 3], ALU.mult)
                            nc.vector.tensor_tensor(qT[s][:], q_ps, table[:, 0], ALU.mult)
                            nc.vector.tensor_tensor(qR[s][:], ps[s][:, 0, 2 * P:3 * P], table[:, 1], ALU.mult).then_inc(qk_products, 1)
                            dve.wait_ge(qk_products, count(i, s))
                            nc.vector.tensor_tensor(kT[s][:], kT[s][:], kR[s][:], ALU.add).then_inc(k_ready, 1)
                            nc.vector.tensor_tensor(qT[s][:], qT[s][:], qR[s][:], ALU.add)
                        else:
                            nc.vector.tensor_scalar(kT[s][:], k_ps, col(k_bias) if k_bias else 0.0, None, ALU.add).then_inc(k_ready, 1)
                            nc.vector.tensor_scalar(qT[s][:], q_ps, col(q_bias) if q_bias else 0.0, SCALE, ALU.add, ALU.mult)
                        nc.vector.tensor_tensor(v_bd[s][:].rearrange("p b g n -> p (b g) n"),
                                                ps[s][:, 1, 0:NB * P].rearrange("p (g n) -> p g n", n=HG * HD),
                                                v_mask[:].unsqueeze(1).broadcast_to([P, NB * NG, HG * HD]),
                                                ALU.mult).then_inc(qkv_ready, 1)
                    for s in per:
                        scores = ps[s][:].rearrange("p a n -> p (a n)")[:, 0:SC].rearrange("p (h k) -> p h k", h=H)
                        dve.wait_ge(scores_in_psum, count(i, s))
                        nc.vector.tensor_reduce(nmax[s][:], scores, AX.X, ALU.max, negate=True).then_inc(max_ready, 1)
                        dve.wait_ge(max_ready, count(i, s))
                        nc.vector.tensor_tensor(probs[s][:], scores, nmax[s][:].unsqueeze(2).broadcast_to([P, H, L]),
                                                ALU.add).then_inc(shifted, 1)
                    for s in per:
                        dve.wait_ge(probs_ready, count(i, s))
                        nc.vector.tensor_reduce(den[s][:], probs[s][:], AX.X, ALU.add).then_inc(den_ready, 1)
                    for s in per:
                        dve.wait_ge(den_ready, count(i, s))
                        nc.vector.reciprocal(rden[s][:], den[s][:]).then_inc(rden_ready, 1)
                    for s in per:
                        dve.wait_ge(rden_ready, count(i, s))
                        dve.wait_ge(att_in_psum, count(i, s))
                        nc.vector.tensor_tensor(att[s][:].rearrange("p (h d) -> p h d", h=H),
                                                ps[s][:, 0, 0:P].rearrange("p (h d) -> p h d", h=H),
                                                rden[s][:].unsqueeze(2).broadcast_to([P, H, HD]), ALU.mult).then_inc(att_ready, 1)
                    for s in per:
                        dve.wait_ge(out_in_psum, count(i, s))
                        if keep_norm:
                            nc.vector.tensor_tensor(y_a[s][:], ps[s][:, 0, 0:P], h[s][:], ALU.add).then_inc(out_a_ready, 1)
                            dve.wait_ge(out_a_ready, count(i, s))
                            nc.vector.tensor_tensor(y_b[s][:], y_a[s][:], x_t[s][:], ALU.add).then_inc(out_ready, 1)
                        else:
                            nc.vector.tensor_tensor(y_a[s][:], ps[s][:, 0, 0:P], x_t[s][:], ALU.add).then_inc(out_ready, 1)

            @block.tensor
            def _(pe):
                pe.wait_ge(weights_loaded, 16 * len(loads))
                pe.wait_ge(consts_ready, 5)
                if alibi:
                    pe.wait_ge(alibi_ready, 1)
                with pe.Fori(0, TILES // SLOTS) as i:
                    for s in per:
                        pe.wait_ge(hn_ready if second_norm else h_ready, count(i, s))
                        nc.tensor.transpose(ps[s][:, 0, 0:P], hn[s][:], ident[:]).then_inc(hT_in_psum, 1)
                    if latent:
                        for s in per:
                            pe.wait_ge(hT_ready, count(i, s))
                            nc.tensor.matmul(ps[s][:, 1, 0:64], hT[s][:], w_lat[:], start=True, stop=True).then_inc(lat_in_psum, 1)
                        for s in per:
                            pe.wait_ge(lat_ready, count(i, s))
                            pe.sem_inc(wait_carried, 1)
                            nc.tensor.transpose(ps[s][0:64, 1, P:2 * P], lat[s][:], ident[:]).then_inc(latT_in_psum, 1)
                    for s in per:
                        pe.wait_ge(hT_ready, count(i, s))
                        if latent:
                            pe.wait_ge(latT_ready, count(i, s))
                            kv = latT[s][:]
                            wk, wkr, wv = wk_lat[:, 0], wk_lat[:, 1], wk_lat[:, 2]
                        else:
                            if ctx is not None:
                                pe.wait_ge(x_loaded[s], i * (16 * LOADS) + 16 * LOADS)
                            kv = c_t[s][:] if ctx is not None else hT[s][:]
                            wk, wkr, wv = w_in[:, 1], w_in[:, 3 if rope else 1], w_in[:, WQK]
                        nc.tensor.matmul(ps[s][:, 0, 0:P], w_in[:, 0], hT[s][:], start=True, stop=True)
                        nc.tensor.matmul(ps[s][:, 0, P:2 * P], wk, kv, start=True, stop=True)
                        if rope:
                            nc.tensor.matmul(ps[s][:, 0, 2 * P:3 * P], w_in[:, 2], hT[s][:], start=True, stop=True)
                            nc.tensor.matmul(ps[s][:, 0, 3 * P:4 * P], wkr, kv, start=True, stop=True)
                        for b in range(NB):
                            for g in range(HG):
                                out = ps[s][g * L:(g + 1) * L, 1, b * P:(b + 1) * P]
                                m = nc.tensor.matmul(out, kv[:, b * L:(b + 1) * L], wv, start=True, stop=not v_bias,
                                                     skip_group_check=True)
                                if v_bias:
                                    m = nc.tensor.matmul(out, ones[:, 0:L], brow[:, ROWS.index(v_bias)],
                                                         start=False, stop=True, skip_group_check=True)
                        m.then_inc(qkv_in_psum, 1)
                    for s in per:
                        pe.wait_ge(qkv_ready, count(i, s))
                        pe.wait_ge(k_spread, count(i, s))
                        for n in range(0, SC, 512):
                            for b in range(NB):
                                out = ps[s][b * L:(b + 1) * L, n // 512, :]
                                if alibi:
                                    nc.tensor.matmul(out, ident[:, b * L:(b + 1) * L], bias_full[:, n:n + 512],
                                                     start=True, stop=False, skip_group_check=True)
                                else:
                                    nc.tensor.matmul(out, ident_b[:, b * L:(b + 1) * L], mask[:, n:n + 512],
                                                     start=True, stop=False, skip_group_check=True)
                                m = nc.tensor.matmul(out, qT[s][:, b * L:(b + 1) * L],
                                                     k_bd[s][:, b].rearrange("p h k -> p (h k)")[:, n:n + 512],
                                                     start=False, stop=True, skip_group_check=True)
                        m.then_inc(scores_in_psum, 1)
                    for s in per:
                        pe.wait_ge(probs_ready, count(i, s))
                        for g in range(NG):
                            m = nc.tensor.transpose(ps[s][:].rearrange("p a n -> p (a n)")[:, g * P:(g + 1) * P],
                                                    probs[s][:, g * HG:(g + 1) * HG].rearrange("p h k -> p (h k)"), ident[:])
                        m.then_inc(probsT_in_psum, 1)
                    for s in per:
                        pe.wait_ge(probsT_ready, count(i, s))
                        for g in range(NG):
                            for b in range(NB):
                                m = nc.tensor.matmul(ps[s][b * L:(b + 1) * L, 0, g * HG * HD:(g + 1) * HG * HD],
                                                     probsT[s][:, g, b * L:(b + 1) * L], v_bd[s][:, b, g],
                                                     start=True, stop=True, skip_group_check=True)
                        m.then_inc(att_in_psum, 1)
                    for s in per:
                        pe.wait_ge(att_ready, count(i, s))
                        nc.tensor.transpose(ps[s][:, 1, 0:P], att[s][:], ident[:]).then_inc(attT_in_psum, 1)
                    for s in per:
                        pe.wait_ge(attT_ready, count(i, s))
                        m = nc.tensor.matmul(ps[s][:, 0, 0:P], attT[s][:], w_out[:], start=True, stop=not o_bias)
                        if o_bias:
                            m = nc.tensor.matmul(ps[s][:, 0, 0:P], ones[:], brow[:, ROWS.index(o_bias)], start=False, stop=True)
                        m.then_inc(out_in_psum, 1)
        end_phase(nc, sems)


def moe_phase(nc, dr, name, *, x_in, base_in, out, E, w1, w2, router, norm, gamma, beta=None, act_func=None,
              b1=None, b2=None, gate_b=None, top=2, by_position=False):
    TC = 4
    CH = TILES // TC
    BLK = 16
    BE = BLK // E
    HB = 4
    with ExitStack() as st:
        def sb(n, shape, dt=F32):
            return st.enter_context(nc.sbuf_tensor(f"{name}_{n}", shape, dt))

        sems = []

        def sem(n):
            sems.append(nc.alloc_semaphore(f"{name}_{n}"))
            return sems[-1]

        w1_s = sb("w1", [P, BLK, P])
        w2_s = sb("w2", [P, BLK, P])
        rt_s = sb("rt", [P, E])
        cols = sb("cols", [P, len(COLS)])
        ident = sb("ident", [P, P])
        b1_s = sb("b1", [P, BLK]) if b1 else None
        b2_s = sb("b2", [1, E * P]) if b2 else None
        gb_s = sb("gb", [1, E]) if gate_b else None
        ones = sb("ones", [1, P])
        half = sb("half", [P, 2, TC])
        iota = sb("iota", [P, 8])
        xa = sb("xa", [P, TC, P])
        base = sb("base", [P, TC, P])
        mom = sb("mom", [P, TC, 6])
        mv = sb("mv", [P, TC, 2])
        rstd = sb("rstd", [P, 2, TC])
        hn = sb("hn", [P, TC, P])
        hT = sb("hT", [P, TC * P])
        lg = sb("lg", [P, TC, 8])
        nmax = sb("nmax", [P, TC])
        den = sb("den", [P, TC])
        rden = sb("rden", [P, TC])
        prob = sb("prob", [P, TC, 8])
        best = sb("best", [P, TC, 8])
        where = sb("where", [P, TC, 8], U32)
        where_f = sb("where_f", [P, TC, 8])
        gates = sb("gates", [P, TC, 8])
        gate2 = sb("gate2", [P, TC, 8])
        hid = sb("hid", [P, BLK, TC * P])
        y = sb("y", [P, TC, P])
        hid_ps = st.enter_context(nc.psum_tensor(f"{name}_hid_ps", [P, HB, 512], F32))
        y_ps = st.enter_context(nc.psum_tensor(f"{name}_y_ps", [P, 2, 2, 512], F32))

        weights_loaded = sem("weights_loaded")
        pool_consts = sem("pool_consts")
        x_loaded = sem("x_loaded")
        base_loaded = sem("base_loaded")
        wait_carried = sem("wait_carried")
        stats_ready = sem("stats_ready")
        moments_ready = sem("moments_ready")
        square_ready = sem("square_ready")
        eps_added = sem("eps_added")
        rstd_ready = sem("rstd_ready")
        hn_ready = sem("hn_ready")
        hT_in_psum = sem("hT_in_psum")
        hT_ready = sem("hT_ready")
        logits_in_psum = sem("logits_in_psum")
        logits_max = sem("logits_max")
        logits_out = sem("logits_out")
        exp_ready = sem("exp_ready")
        den_ready = sem("den_ready")
        rden_ready = sem("rden_ready")
        prob_ready = sem("prob_ready")
        best_ready = sem("best_ready")
        where_ready = sem("where_ready")
        where_cast = sem("where_cast")
        gate_parts = sem("gate_parts")
        gates_ready = sem("gates_ready")
        hid_in_psum = sem("hid_in_psum")
        hid_ready = sem("hid_ready")
        y_in_psum = sem("y_in_psum")
        y_used = sem("y_used")
        y_sum = sem("y_sum")
        stored = sem("stored")

        loads = [(w1_s, dr[w1]), (w2_s, dr[w2]), (rt_s, dr[router]), (cols, dr["cols"]), (ident, dr["ident"]), (iota, dr["iota"])]
        if b1:
            loads += [(b1_s, dr[b1]), (b2_s, dr[b2]), (gb_s, dr[gate_b])]
        xv = x_in.rearrange("(i t p) d -> i p t d", t=TC, p=P)
        bv = base_in.rearrange("(i t p) d -> i p t d", t=TC, p=P)
        ov = tiles_by_position(out) if by_position else tiles_by_batch(out)
        STORES = TC * (P // B if by_position else 1)

        def col(n):
            return cols[:, COLS.index(n):COLS.index(n) + 1]

        with nc.Block() as block:
            @block.sync
            def _(sp):
                for dst, src in loads:
                    sp.dma_start(dst[:], src).then_inc(weights_loaded, 16)
                with sp.Fori(0, CH) as i:
                    sp.wait_ge(stored, i * (16 * STORES) + 1)
                    sp.dma_start(xa[:], xv[i]).then_inc(x_loaded, 16)
                    sp.dma_start(base[:], bv[i]).then_inc(base_loaded, 16)
                    for t in range(TC):
                        sp.wait_ge(y_used, i * TC + t + 3)
                        if by_position:
                            for q in range(P // B):
                                sp.dma_start(ov[i * TC + t, q], y[q * B:(q + 1) * B, t]).then_inc(stored, 16)
                        else:
                            sp.dma_start(ov[i * TC + t], y[:, t]).then_inc(stored, 16)
                sp.wait_ge(stored, CH * 16 * STORES + 1)

            @block.gpsimd
            def _(pool):
                pool.sem_inc(stored, 1)
                nc.gpsimd.memset(ones[:], 1.0).then_inc(pool_consts, 1)
                nc.gpsimd.memset(lg[:], -3.0e38).then_inc(pool_consts, 1)
                nc.gpsimd.memset(half[:, 0], -0.5).then_inc(pool_consts, 1)
                nc.gpsimd.memset(half[:, 1], 1e-6 if norm == "rms" else 1e-5).then_inc(pool_consts, 1)
                pool.wait_ge(pool_consts, 4)
                with pool.Fori(0, CH) as i:
                    if norm == "rms":
                        pool.wait_ge(square_ready, i + 1)
                    else:
                        pool.wait_ge(moments_ready, i * TC + TC)
                    nc.gpsimd.tensor_tensor(rstd[:, 0], mv[:, :, 1], half[:, 1], ALU.add).then_inc(eps_added, 1)
                    pool.wait_ge(eps_added, i + 1)
                    nc.gpsimd.tensor_tensor(rstd[:, 1], rstd[:, 0], half[:, 0], ALU.pow).then_inc(rstd_ready, 1)

            @block.scalar
            def _(act):
                act.wait_ge(weights_loaded, 16 * len(loads))
                with act.Fori(0, CH) as i:
                    act.wait_ge(hT_in_psum, i + 1)
                    nc.scalar.activation(hT[:], hid_ps[:, 0], ACT.Identity, scale=col(gamma),
                                         bias=col(beta) if beta else 0.0).then_inc(hT_ready, 1)
                    if top == 2:
                        act.wait_ge(logits_out, i + 1)
                        nc.scalar.activation(lg[:], lg[:], ACT.Exp).then_inc(exp_ready, 1)
                    for n in range(BLK):
                        act.wait_ge(hid_in_psum, i * BLK + n + 1)
                        nc.scalar.activation(hid[:, n], hid_ps[:, n % HB], act_func,
                                             bias=b1_s[:, n:n + 1] if b1 else 0.0).then_inc(hid_ready, 1)

            @block.vector
            def _(dve):
                dve.sem_inc(y_used, 2)
                dve.wait_ge(weights_loaded, 16 * len(loads))
                dve.wait_ge(pool_consts, 4)
                with dve.Fori(0, CH) as i:
                    dve.wait_ge(x_loaded, i * 16 + 16)
                    for t in range(TC):
                        nc.vector.bn_stats(mom[:, t], xa[:, t]).then_inc(stats_ready, 1)
                    for t in range(TC):
                        dve.wait_ge(stats_ready, i * TC + t + 1)
                        dve.sem_inc(wait_carried, 1)
                        nc.vector.bn_aggr(mv[:, t], mom[:, t]).then_inc(moments_ready, 1)
                    if norm == "rms":
                        for t in range(TC):
                            dve.wait_ge(moments_ready, i * TC + t + 1)
                            m = nc.vector.scalar_tensor_tensor(mv[:, t, 1:2], mv[:, t, 0:1], mv[:, t, 0:1], mv[:, t, 1:2],
                                                               ALU.mult, ALU.add)
                        m.then_inc(square_ready, 1)
                    dve.wait_ge(rstd_ready, i + 1)
                    for t in range(TC):
                        if norm == "rms":
                            nc.vector.tensor_scalar(hn[:, t], xa[:, t], rstd[:, 1, t:t + 1], None, ALU.mult).then_inc(hn_ready, 1)
                        else:
                            nc.vector.tensor_scalar(hn[:, t], xa[:, t], mv[:, t, 0:1], rstd[:, 1, t:t + 1],
                                                    ALU.subtract, ALU.mult).then_inc(hn_ready, 1)
                    dve.wait_ge(logits_in_psum, i + 1)
                    logits = y_ps[:, 1, 0, 0:TC * E].rearrange("p (t e) -> p t e", e=E)
                    if top == 2:
                        nc.vector.tensor_reduce(nmax[:], logits, AX.X, ALU.max, negate=True).then_inc(logits_max, 1)
                        dve.wait_ge(logits_max, i + 1)
                        nc.vector.tensor_tensor(lg[:], logits, nmax[:].unsqueeze(2).broadcast_to([P, TC, 8]),
                                                ALU.add).then_inc(logits_out, 1)
                        dve.wait_ge(exp_ready, i + 1)
                        nc.vector.tensor_reduce(den[:], lg[:], AX.X, ALU.add).then_inc(den_ready, 1)
                        dve.wait_ge(den_ready, i + 1)
                        nc.vector.reciprocal(rden[:], den[:]).then_inc(rden_ready, 1)
                        dve.wait_ge(rden_ready, i + 1)
                        nc.vector.tensor_tensor(prob[:], lg[:], rden[:].unsqueeze(2).broadcast_to([P, TC, 8]),
                                                ALU.mult).then_inc(prob_ready, 1)
                        dve.wait_ge(prob_ready, i + 1)
                        ranked = prob
                    else:
                        nc.vector.tensor_copy(lg[:, :, 0:E], logits).then_inc(logits_out, 1)
                        dve.wait_ge(logits_out, i + 1)
                        ranked = lg
                    for t in range(TC):
                        dve.sem_inc(wait_carried, 1)
                        nc.vector.max(best[:, t], ranked[:, t]).then_inc(best_ready, 1)
                    for t in range(TC):
                        dve.wait_ge(best_ready, i * TC + t + 1)
                        dve.sem_inc(wait_carried, 1)
                        nc.vector.max_index(where[:, t], best[:, t], ranked[:, t]).then_inc(where_ready, 1)
                    dve.wait_ge(where_ready, i * TC + TC)
                    nc.vector.tensor_copy(where_f[:], where[:]).then_inc(where_cast, 1)
                    dve.wait_ge(where_cast, i + 1)
                    for t in range(TC):
                        if top == 2:
                            nc.vector.tensor_scalar(gates[:, t], iota[:], where_f[:, t, 0:1], best[:, t, 0:1],
                                                    ALU.is_equal, ALU.mult)
                            m = nc.vector.tensor_scalar(gate2[:, t], iota[:], where_f[:, t, 1:2], best[:, t, 1:2],
                                                        ALU.is_equal, ALU.mult)
                        else:
                            m = nc.vector.tensor_scalar(gates[:, t], iota[:], where_f[:, t, 0:1], None, ALU.is_equal)
                    m.then_inc(gate_parts, 1)
                    dve.wait_ge(gate_parts, i + 1)
                    if top == 2:
                        nc.vector.tensor_tensor(gates[:], gates[:], gate2[:], ALU.add).then_inc(gates_ready, 1)
                        dve.wait_ge(gates_ready, i + 1)
                    dve.wait_ge(base_loaded, i * 16 + 16)
                    for t in range(TC):
                        dve.wait_ge(y_in_psum, i * TC + t + 1)
                        ye = y_ps[:, t % 2].rearrange("p a n -> p (a n)")[:, 0:E * P].rearrange("p (e d) -> p e d", e=E)
                        for e in range(E):
                            if e:
                                dve.wait_ge(y_sum, i * (TC * (E - 1)) + t * (E - 1) + e)
                            m = nc.vector.scalar_tensor_tensor(y[:, t], ye[:, e], gates[:, t, e:e + 1],
                                                               y[:, t] if e else base[:, t], ALU.mult, ALU.add)
                            m.then_inc(y_used if e == E - 1 else y_sum, 1)

            @block.tensor
            def _(pe):
                pe.wait_ge(weights_loaded, 16 * len(loads))
                pe.wait_ge(pool_consts, 4)
                with pe.Fori(0, CH) as i:
                    for t in range(TC):
                        pe.wait_ge(hn_ready, i * TC + t + 1)
                        m = nc.tensor.transpose(hid_ps[:, 0, t * P:(t + 1) * P], hn[:, t], ident[:])
                    m.then_inc(hT_in_psum, 1)
                    pe.wait_ge(hT_ready, i + 1)
                    pe.wait_ge(y_used, i * TC + 2)
                    for t in range(TC):
                        lo = y_ps[:, 1, 0, t * E:(t + 1) * E]
                        m = nc.tensor.matmul(lo, hT[:, t * P:(t + 1) * P], rt_s[:], start=True, stop=not gate_b)
                        if gate_b:
                            m = nc.tensor.matmul(lo, ones[:], gb_s[:], start=False, stop=True)
                    m.then_inc(logits_in_psum, 1)
                    for n in range(BLK):
                        if n >= HB:
                            pe.wait_ge(hid_ready, i * BLK + n - HB + 1)
                        nc.tensor.matmul(hid_ps[:, n % HB], w1_s[:, n], hT[:], start=True, stop=True).then_inc(hid_in_psum, 1)
                    pe.wait_ge(hid_ready, i * BLK + BLK)
                    pe.wait_ge(logits_out, i + 1)
                    for t in range(TC):
                        pe.wait_ge(y_used, i * TC + t + 1)
                        yf = y_ps[:, t % 2].rearrange("p a n -> p (a n)")
                        for e in range(E):
                            if b2:
                                nc.tensor.matmul(yf[:, e * P:(e + 1) * P], ones[:], b2_s[:, e * P:(e + 1) * P],
                                                 start=True, stop=False, skip_group_check=True)
                            for k in range(BE):
                                n = e * BE + k
                                m = nc.tensor.matmul(yf[:, e * P:(e + 1) * P], hid[:, n, t * P:(t + 1) * P], w2_s[:, n],
                                                     start=k == 0 and not b2, stop=k == BE - 1, skip_group_check=True)
                        m.then_inc(y_in_psum, 1)
        end_phase(nc, sems)


def state_space_phase(nc, dr, name, *, x_in, out):
    TC = 4
    CH = TILES // TC
    NB = B // CH
    W = TC * P
    TAPS = 4
    ROUNDS = 6
    with ExitStack() as st:
        def sb(n, shape, dt=F32):
            return st.enter_context(nc.sbuf_tensor(f"{name}_{n}", shape, dt))

        sems = []

        def sem(n):
            sems.append(nc.alloc_semaphore(f"{name}_{n}"))
            return sems[-1]

        w_in = sb("w_in", [P, 4, P])
        w_out = sb("w_out", [P, 2, P])
        w_b = sb("w_b", [P, 2, 32])
        w_c = sb("w_c", [P, 4, 2, P])
        a_pow = sb("a_pow", [P, ROUNDS, P])
        at_pow = sb("at_pow", [P, ROUNDS, P])
        taps = sb("taps", [P, 2, TAPS])
        cols = sb("cols", [P, len(COLS)])
        ident = sb("ident", [P, P])
        half = sb("half", [P, 2, TC])
        x_t = sb("x", [P, TC, P])
        mom = sb("mom", [P, TC, 6])
        mv = sb("mv", [P, TC, 2])
        rstd = sb("rstd", [P, 2, TC])
        mom2 = sb("mom2", [P, TC, 6])
        mv2 = sb("mv2", [P, TC, 2])
        rstd2 = sb("rstd2", [P, 2, TC])
        h = sb("h", [P, TC, P])
        hn = sb("hn", [P, TC, P])
        hT = sb("hT", [P, W])
        x_plus_h = sb("x_plus_h", [P, TILES, P])
        xp = sb("xp", [P, 2, CH, W])
        conv = sb("conv", [P, 2, CH, W])
        sig_c = sb("sig_c", [P, 2, W])
        sig_z = sb("sig_z", [P, 2, CH, W])
        state = sb("state", [P, NB, S])
        mix = sb("mix", [P, 2, W])
        y = sb("y", [P, 2, W])
        o = sb("o", [P, 2, TC, P])
        pj = st.enter_context(nc.psum_tensor(f"{name}_pj", [P, 4, 512], F32))
        pt = st.enter_context(nc.psum_tensor(f"{name}_pt", [P, 512], F32))
        pv = st.enter_context(nc.psum_tensor(f"{name}_pv", [P, 512], F32))
        pa = st.enter_context(nc.psum_tensor(f"{name}_pa", [P, 2, P], F32))
        po = st.enter_context(nc.psum_tensor(f"{name}_po", [P, 512], F32))

        weights_loaded = sem("weights_loaded")
        pool_consts = sem("pool_consts")
        x_loaded = sem("x_loaded")
        wait_carried = sem("wait_carried")
        stats_ready = sem("stats_ready")
        moments_ready = sem("moments_ready")
        eps_added = sem("eps_added")
        rstd_ready = sem("rstd_ready")
        h_ready = sem("h_ready")
        stats2_ready = sem("stats2_ready")
        moments2_ready = sem("moments2_ready")
        eps2_added = sem("eps2_added")
        rstd2_ready = sem("rstd2_ready")
        hn_ready = sem("hn_ready")
        x_used = sem("x_used")
        hT_in_psum = sem("hT_in_psum")
        hT_ready = sem("hT_ready")
        xz_in_psum = sem("xz_in_psum")
        x_part_ready = sem("x_part_ready")
        sig_z_ready = sem("sig_z_ready")
        tap_added = sem("tap_added")
        conv_ready = sem("conv_ready")
        sig_c_ready = sem("sig_c_ready")
        silu_ready = sem("silu_ready")
        power_in_psum = sem("power_in_psum")
        power_ready = sem("power_ready")
        bu_in_psum = sem("bu_in_psum")
        share_in_psum = sem("share_in_psum")
        state_ready = sem("state_ready")
        cs_in_psum = sem("cs_in_psum")
        mix_ready = sem("mix_ready")
        y_ready = sem("y_ready")
        out_in_psum = sem("out_in_psum")
        out_ready = sem("out_ready")
        stored = [sem(f"stored{n}") for n in range(2)]

        loads = [(w_in[:], dr["ssm_w_in"]), (w_out[:], dr["ssm_w_out"]), (w_b[:], dr["ssm_b"]), (w_c[:], dr["ssm_c"]),
                 (a_pow[:, 0], dr["ssm_a"]), (at_pow[:, 0], dr["ssm_at"]), (taps[:], dr["ssm_taps"]),
                 (cols[:], dr["cols"]), (ident[:], dr["ident"])]
        xv = x_in.rearrange("(i t p) d -> i p t d", t=TC, p=P)
        ov = out.rearrange("(i t p) d -> i p t d", t=TC, p=P)

        def col(n):
            return cols[:, COLS.index(n):COLS.index(n) + 1]

        with nc.Block() as block:
            @block.sync
            def _(sp):
                for dst, src in loads:
                    sp.dma_start(dst, src).then_inc(weights_loaded, 16)
                with sp.Fori(0, CH) as i:
                    sp.wait_ge(x_used, i * TC + 1)
                    sp.sem_inc(wait_carried, 1)
                    sp.wait_ge(hT_in_psum, i + 1)
                    sp.dma_start(x_t[:], xv[i]).then_inc(x_loaded, 16)
                for j in range(CH):
                    sp.wait_ge(out_ready, j + 1)
                    sp.dma_start(ov[j], o[:, j % 2]).then_inc(stored[j % 2], 16)
                for n in range(2):
                    sp.wait_ge(stored[n], 16 * (CH // 2))

            @block.gpsimd
            def _(pool):
                nc.gpsimd.memset(half[:, 0], -0.5).then_inc(pool_consts, 1)
                nc.gpsimd.memset(half[:, 1], 1e-5).then_inc(pool_consts, 1)
                pool.wait_ge(pool_consts, 2)
                with pool.Fori(0, CH) as i:
                    pool.wait_ge(moments_ready, i * TC + TC)
                    nc.gpsimd.tensor_tensor(rstd[:, 0], mv[:, :, 1], half[:, 1], ALU.add).then_inc(eps_added, 1)
                    pool.wait_ge(eps_added, i + 1)
                    nc.gpsimd.tensor_tensor(rstd[:, 1], rstd[:, 0], half[:, 0], ALU.pow).then_inc(rstd_ready, 1)
                    pool.wait_ge(moments2_ready, i * TC + TC)
                    nc.gpsimd.tensor_tensor(rstd2[:, 0], mv2[:, :, 1], half[:, 1], ALU.add).then_inc(eps2_added, 1)
                    pool.wait_ge(eps2_added, i + 1)
                    nc.gpsimd.tensor_tensor(rstd2[:, 1], rstd2[:, 0], half[:, 0], ALU.pow).then_inc(rstd2_ready, 1)

            @block.scalar
            def _(act):
                act.wait_ge(weights_loaded, 16 * len(loads))
                with act.Fori(0, CH) as i:
                    act.wait_ge(hT_in_psum, i + 2)
                    nc.scalar.activation(hT[:], pt[:], ACT.Identity, scale=col("L0_attn_ln_gamma"),
                                         bias=col("L0_attn_ln_beta")).then_inc(hT_ready, 1)
                    for n in range(2):
                        act.wait_ge(xz_in_psum, i * 4 + n + 1)
                        nc.scalar.activation(xp[:, n, bass.ds(i, 1)].rearrange("p a w -> p (a w)"), pj[:, n],
                                             ACT.Identity).then_inc(x_part_ready, 1)
                    for n in range(2):
                        act.wait_ge(xz_in_psum, i * 4 + n + 3)
                        nc.scalar.activation(sig_z[:, n, bass.ds(i, 1)].rearrange("p a w -> p (a w)"), pj[:, 2 + n],
                                             ACT.Sigmoid).then_inc(sig_z_ready, 1)
                for j in range(CH):
                    for n in range(2):
                        act.wait_ge(conv_ready, 2 * j + n + 1)
                        if j:
                            act.wait_ge(silu_ready, 2 * (j - 1) + n + 1)
                        nc.scalar.activation(sig_c[:, n], conv[:, n, j], ACT.Sigmoid).then_inc(sig_c_ready, 1)

            @block.vector
            def _(dve):
                dve.sem_inc(x_used, 1)
                dve.wait_ge(weights_loaded, 16 * len(loads))
                with dve.Fori(0, CH) as i:
                    dve.wait_ge(x_loaded, i * 16 + 16)
                    for t in range(TC):
                        nc.vector.bn_stats(mom[:, t], x_t[:, t]).then_inc(stats_ready, 1)
                    for t in range(TC):
                        dve.wait_ge(stats_ready, i * TC + t + 1)
                        dve.sem_inc(wait_carried, 1)
                        nc.vector.bn_aggr(mv[:, t], mom[:, t]).then_inc(moments_ready, 1)
                    dve.wait_ge(rstd_ready, i + 1)
                    for t in range(TC):
                        nc.vector.tensor_scalar(h[:, t], x_t[:, t], mv[:, t, 0:1], rstd[:, 1, t:t + 1],
                                                ALU.subtract, ALU.mult).then_inc(h_ready, 1)
                    for t in range(TC):
                        dve.wait_ge(h_ready, i * TC + t + 1)
                        nc.vector.bn_stats(mom2[:, t], h[:, t]).then_inc(stats2_ready, 1)
                    for t in range(TC):
                        dve.wait_ge(stats2_ready, i * TC + t + 1)
                        dve.sem_inc(wait_carried, 1)
                        nc.vector.bn_aggr(mv2[:, t], mom2[:, t]).then_inc(moments2_ready, 1)
                    for t in range(TC):
                        nc.vector.tensor_tensor(x_plus_h[:, bass.ds(i * TC + t, 1)].rearrange("p a d -> p (a d)"),
                                                x_t[:, t], h[:, t], ALU.add).then_inc(x_used, 1)
                    dve.wait_ge(rstd2_ready, i + 1)
                    for t in range(TC):
                        nc.vector.tensor_scalar(hn[:, t], h[:, t], mv2[:, t, 0:1], rstd2[:, 1, t:t + 1],
                                                ALU.subtract, ALU.mult).then_inc(hn_ready, 1)
                for k in range(1, ROUNDS):
                    dve.wait_ge(power_in_psum, k)
                    nc.vector.tensor_copy(a_pow[:, k], pa[:, 0])
                    nc.vector.tensor_copy(at_pow[:, k], pa[:, 1]).then_inc(power_ready, 1)
                dve.wait_ge(bu_in_psum, 1)
                nc.vector.tensor_copy(state[:].rearrange("p b t -> p (b t)"), pv[:]).then_inc(state_ready, 1)

                work = [(j, n) for j in range(CH) for n in range(2)]
                dve.wait_ge(x_part_ready, 2 * CH)
                for m, (j, n) in enumerate(work):
                    src = xp[:, n, j].rearrange("p (b t) -> p b t", t=S)
                    dst = conv[:, n, j].rearrange("p (b t) -> p b t", t=S)
                    nc.vector.tensor_scalar(dst, src, taps[:, n, TAPS - 1:TAPS], col(f"conv_b{n}"),
                                            ALU.mult, ALU.add).then_inc(tap_added, 1)
                    for k in range(1, TAPS):
                        dve.wait_ge(tap_added, m * (TAPS - 1) + k)
                        nc.vector.scalar_tensor_tensor(dst[:, :, k:], src[:, :, 0:S - k], taps[:, n, TAPS - 1 - k:TAPS - k],
                                                       dst[:, :, k:], ALU.mult, ALU.add)\
                            .then_inc(tap_added if k < TAPS - 1 else conv_ready, 1)
                    if m < ROUNDS:
                        k = 1 << m
                        dve.wait_ge(share_in_psum, m + 1)
                        dve.wait_ge(state_ready, m + 1)
                        nc.vector.tensor_tensor(state[:, :, k:], state[:, :, k:],
                                                pv[:, 0:NB * (S - k)].rearrange("p (b t) -> p b t", b=NB),
                                                ALU.add).then_inc(state_ready, 1)
                    if m:
                        a, c = work[m - 1]
                        dve.wait_ge(sig_c_ready, m)
                        nc.vector.tensor_tensor(conv[:, c, a], conv[:, c, a], sig_c[:, c], ALU.mult).then_inc(silu_ready, 1)
                dve.wait_ge(sig_c_ready, 2 * CH)
                nc.vector.tensor_tensor(conv[:, 1, CH - 1], conv[:, 1, CH - 1], sig_c[:, 1], ALU.mult).then_inc(silu_ready, 1)
                dve.wait_ge(silu_ready, 2 * CH)
                dve.wait_ge(sig_z_ready, 2 * CH)
                for j in range(CH):
                    for n in range(2):
                        dve.wait_ge(cs_in_psum, 2 * j + n + 1)
                        nc.vector.tensor_tensor(mix[:, n], pj[:, 2 * (j % 2) + n], conv[:, n, j], ALU.add).then_inc(mix_ready, 1)
                    if j:
                        dve.wait_ge(out_in_psum, j)
                    for n in range(2):
                        dve.wait_ge(mix_ready, 2 * j + n + 1)
                        nc.vector.tensor_tensor(y[:, n], mix[:, n], sig_z[:, n, j], ALU.mult).then_inc(y_ready, 1)
                    dve.wait_ge(out_in_psum, j + 1)
                    if j >= 2:
                        dve.wait_ge(stored[j % 2], 16 * (j // 2))
                    nc.vector.tensor_tensor(o[:, j % 2].rearrange("p t d -> p (t d)"), po[:],
                                            x_plus_h[:, j * TC:(j + 1) * TC].rearrange("p t d -> p (t d)"),
                                            ALU.add).then_inc(out_ready, 1)

            @block.tensor
            def _(pe):
                pe.sem_inc(hT_in_psum, 1)
                pe.wait_ge(weights_loaded, 16 * len(loads))
                with pe.Fori(0, CH) as i:
                    for t in range(TC):
                        pe.wait_ge(hn_ready, i * TC + t + 1)
                        m = nc.tensor.transpose(pt[:, t * P:(t + 1) * P], hn[:, t], ident[:])
                    m.then_inc(hT_in_psum, 1)
                    pe.wait_ge(hT_ready, i + 1)
                    for n in range(4):
                        nc.tensor.matmul(pj[:, n], w_in[:, n], hT[:], start=True, stop=True).then_inc(xz_in_psum, 1)
                    pe.wait_ge(sig_z_ready, i * 2 + 2)
                for k in range(1, ROUNDS):
                    if k > 1:
                        pe.wait_ge(power_ready, k - 1)
                    nc.tensor.matmul(pa[:, 0], at_pow[:, k - 1], a_pow[:, k - 1], start=True, stop=True, skip_group_check=True)
                    nc.tensor.matmul(pa[:, 1], a_pow[:, k - 1], at_pow[:, k - 1], start=True, stop=True,
                                     skip_group_check=True).then_inc(power_in_psum, 1)
                pe.wait_ge(x_part_ready, 2 * CH)
                for j in range(CH):
                    for n in range(2):
                        m = nc.tensor.matmul(pv[32 * j:32 * j + 32], w_b[:, n], xp[:, n, j], start=n == 0, stop=n == 1,
                                             skip_group_check=True)
                m.then_inc(bu_in_psum, 1)
                pe.wait_ge(power_ready, ROUNDS - 1)
                for k in range(ROUNDS):
                    n = 1 << k
                    pe.wait_ge(state_ready, k + 1)
                    nc.tensor.matmul(pv[:, 0:NB * (S - n)], at_pow[:, k], state[:, :, 0:S - n], start=True, stop=True).then_inc(share_in_psum, 1)
                pe.wait_ge(state_ready, ROUNDS + 1)
                for j in range(CH):
                    for n in range(2):
                        if j >= 2:
                            pe.wait_ge(mix_ready, 2 * (j - 2) + n + 1)
                        nc.tensor.matmul(pj[:, 2 * (j % 2) + n], w_c[:, j, n], state[:].rearrange("p b t -> p (b t)"),
                                         start=True, stop=True).then_inc(cs_in_psum, 1)
                    pe.wait_ge(y_ready, 2 * j + 2)
                    if j:
                        pe.wait_ge(out_ready, j)
                    for t in range(TC):
                        for n in range(2):
                            m = nc.tensor.matmul(po[:, t * P:(t + 1) * P], y[:, n, t * P:(t + 1) * P], w_out[:, n],
                                                 start=n == 0, stop=n == 1, skip_group_check=True)
                    m.then_inc(out_in_psum, 1)
        end_phase(nc, sems)


def cross_attention_phase(nc, dr, name, *, x_in, out):
    TC, CH = 4, 4
    CK = [(c * 400, 400 if c < 3 else KEYS - 1200) for c in range(4)]
    KT = [(t * P, min(P, KEYS - t * P)) for t in range(-(-KEYS // P))]
    NT = len(KT)
    NC = len(CK)
    VG = [KT[g:g + 4] for g in range(0, NT, 4)]
    PAIRS = H // 2
    Q = 2 * S
    VW = 32
    BLOCKS = 4
    BC = H // BLOCKS * S
    MAX_ROW = 64
    KR = MAX_ROW + PAIRS
    PER_BATCH = 16 * 2 * 2 * BLOCKS
    HALVES = [(0, 800), (800, KEYS - 800)]
    UNITS = PAIRS * NC
    units = [("A", u) for u in range(UNITS)]
    PLAN = [[("K", 0)], units[0:4] + [("V", 0)], units[4:7] + [("K", 1)], units[7:11] + [("V", 1)],
            [("K", 2)] + units[11:14] + [("K", 3)], units[14:17], [("V", 2)] + units[17:21], [("V", 3)] + units[21:25],
            [("D", 0)] + units[25:26], units[26:29], [("O", 0)] + units[29:32], [("M", 0)], []]
    assert len(PLAN) == NT and sum(k == "A" for s in PLAN for k, _ in s) == UNITS

    with ExitStack() as st:
        def sb(n, shape, dt=F32, to=None):
            return (to or st).enter_context(nc.sbuf_tensor(f"{name}_{n}", shape, dt))

        sems, sems1 = [], []

        def sem(n, to=sems):
            to.append(nc.alloc_semaphore(f"{name}_{n}"))
            return to[-1]

        w_kv = sb("w_kv", [P, 2, P])
        cols = sb("cols", [P, len(COLS)])
        ident = sb("ident", [P, P])
        w_o = sb("w_o", [P, 2, 2, P])
        head_mask = sb("head_mask", [P, H])
        q_all = sb("q_all", [P, T])
        q_twice = sb("q_twice", [P, BLOCKS, T // 2])
        x_res = sb("x_res", [P, TILES, P])

        with ExitStack() as s1:
            def sb1(n, shape, dt=F32):
                return sb(n, shape, dt, s1)

            def sem1(n):
                return sem(n, sems1)

            w_q = sb1("w_q", [P, P])
            w_q2 = sb1("w_q2", [P, BLOCKS, 64])
            bq2 = sb1("bq2", [P, BLOCKS])
            w_ot = sb1("w_ot", [P, P])
            brow = sb1("brow", [1, len(ROWS), P])
            ones = sb1("ones", [1, P])
            half = sb1("half", [P, 2, TC])
            bv_wide = sb1("bv_wide", [P, P])
            o_bias = sb1("o_bias", [P, P])
            x_t = sb1("x", [P, TC, P])
            mom = sb1("mom", [P, TC, 6])
            mv = sb1("mv", [P, TC, 2])
            rstd = sb1("rstd", [P, 2, TC])
            h = sb1("h", [P, TC, P])
            hT = sb1("hT", [P, TC * P])
            ph = s1.enter_context(nc.psum_tensor(f"{name}_ph", [P, 512], F32))
            pq = s1.enter_context(nc.psum_tensor(f"{name}_pq", [P, 512], F32))
            pb = s1.enter_context(nc.psum_tensor(f"{name}_pb", [P, 512], F32))
            pq2 = s1.enter_context(nc.psum_tensor(f"{name}_pq2", [P, BLOCKS, TC * S], F32))
            q_weights_loaded = sem1("q_weights_loaded")
            pool_consts = sem1("pool_consts")
            bv_spread = sem1("bv_spread")
            o_bias_in_psum = sem1("o_bias_in_psum")
            o_bias_ready = sem1("o_bias_ready")
            x_loaded = sem1("x_loaded")
            wait_carried = sem1("projection_wait_carried")
            stats_ready = sem1("stats_ready")
            moments_ready = sem1("moments_ready")
            eps_added = sem1("eps_added")
            rstd_ready = sem1("rstd_ready")
            h_ready = sem1("h_ready")
            hT_in_psum = sem1("hT_in_psum")
            hT_ready = sem1("hT_ready")
            q_in_psum = sem1("q_in_psum")
            q_ready = sem1("q_ready")
            q2_in_psum = sem1("q2_in_psum")
            loads = [(w_q, dr["w_q4"]), (w_q2, dr["w_q4_twice"]), (bq2, dr["bq4_twice"]), (w_ot, dr["w_o4"]), (w_kv, dr["w_kv4"]), (cols, dr["cols"]), (ident, dr["ident"]),
                     (w_o, dr["w_o4_pad"]), (head_mask, dr["head_mask"]), (brow, dr["rows"])]
            xv = x_in.rearrange("(i t p) d -> i p t d", t=TC, p=P)

            def col(n):
                return cols[:, COLS.index(n):COLS.index(n) + 1]

            with nc.Block() as block:
                @block.sync
                def _(sp):
                    for dst, src in loads:
                        sp.dma_start(dst[:], src).then_inc(q_weights_loaded, 16)
                    with sp.Fori(0, CH) as i:
                        sp.wait_ge(q_ready, i + 1)
                        sp.dma_start(x_t[:], xv[i]).then_inc(x_loaded, 16)

                @block.gpsimd
                def _(pool):
                    nc.gpsimd.memset(half[:, 0], -0.5).then_inc(pool_consts, 1)
                    nc.gpsimd.memset(half[:, 1], 1e-5).then_inc(pool_consts, 1)
                    nc.gpsimd.memset(ones[:], 1.0).then_inc(pool_consts, 1)
                    nc.gpsimd.memset(bv_wide[:], 1.0).then_inc(pool_consts, 1)
                    pool.wait_ge(pool_consts, 4)
                    with pool.Fori(0, CH) as i:
                        pool.wait_ge(moments_ready, i * TC + TC)
                        nc.gpsimd.tensor_tensor(rstd[:, 0], mv[:, :, 1], half[:, 1], ALU.add).then_inc(eps_added, 1)
                        pool.wait_ge(eps_added, i + 1)
                        nc.gpsimd.tensor_tensor(rstd[:, 1], rstd[:, 0], half[:, 0], ALU.pow).then_inc(rstd_ready, 1)

                @block.scalar
                def _(act):
                    with act.Fori(0, CH) as i:
                        act.wait_ge(hT_in_psum, i + 1)
                        nc.scalar.activation(hT[:], ph[:], ACT.Copy).then_inc(hT_ready, 1)

                @block.vector
                def _(dve):
                    dve.sem_inc(q_ready, 1)
                    dve.wait_ge(q_weights_loaded, 16 * len(loads))
                    dve.wait_ge(pool_consts, 4)
                    nc.vector.tensor_scalar(bv_wide[:], bv_wide[:], col("L1_xattn_bv"), None, ALU.mult).then_inc(bv_spread, 1)
                    dve.wait_ge(o_bias_in_psum, 1)
                    nc.vector.tensor_copy(o_bias[:], pb[:, 0:P]).then_inc(o_bias_ready, 1)
                    dve.wait_ge(o_bias_ready, 1)
                    with dve.Fori(0, CH) as i:
                        dve.wait_ge(x_loaded, i * 16 + 16)
                        for t in range(TC):
                            nc.vector.bn_stats(mom[:, t], x_t[:, t]).then_inc(stats_ready, 1)
                        for t in range(TC):
                            dve.wait_ge(stats_ready, i * TC + t + 1)
                            dve.sem_inc(wait_carried, 1)
                            nc.vector.bn_aggr(mv[:, t], mom[:, t]).then_inc(moments_ready, 1)
                        for t in range(TC):
                            nc.vector.tensor_tensor(x_res[:, bass.ds(i * TC + t, 1)].rearrange("p a d -> p (a d)"),
                                                    x_t[:, t], o_bias[:], ALU.add)
                        dve.wait_ge(rstd_ready, i + 1)
                        for t in range(TC):
                            nc.vector.tensor_scalar(h[:, t], x_t[:, t], mv[:, t, 0:1], rstd[:, 1, t:t + 1],
                                                    ALU.subtract, ALU.mult).then_inc(h_ready, 1)
                        dve.wait_ge(q_in_psum, i + 1)
                        nc.vector.tensor_scalar(q_all[:, bass.ds(i * (TC * P), TC * P)], pq[:], col("L1_xattn_bq"), SCALE,
                                                ALU.add, ALU.mult)
                        dve.wait_ge(q2_in_psum, i + 1)
                        for blk in range(BLOCKS):
                            m = nc.vector.tensor_scalar(q_twice[:, blk, bass.ds(i * (TC * S), TC * S)], pq2[:, blk],
                                                        bq2[:, blk:blk + 1], SCALE, ALU.add, ALU.mult)
                        m.then_inc(q_ready, 1)

                @block.tensor
                def _(pe):
                    pe.wait_ge(q_weights_loaded, 16 * len(loads))
                    pe.wait_ge(pool_consts, 4)
                    pe.wait_ge(bv_spread, 1)
                    nc.tensor.matmul(pb[:, 0:P], bv_wide[:], w_ot[:], start=True, stop=False)
                    nc.tensor.matmul(pb[:, 0:P], ones[:], brow[:, ROWS.index("L1_xattn_bo")], start=False, stop=True).then_inc(o_bias_in_psum, 1)
                    with pe.Fori(0, CH) as i:
                        for t in range(TC):
                            pe.wait_ge(h_ready, i * TC + t + 1)
                            m = nc.tensor.transpose(ph[:, t * P:(t + 1) * P], h[:, t], ident[:])
                        m.then_inc(hT_in_psum, 1)
                        pe.wait_ge(hT_ready, i + 1)
                        nc.tensor.matmul(pq[:], w_q[:], hT[:], start=True, stop=True).then_inc(q_in_psum, 1)
                        by_parity = hT[:].rearrange("p (t a q) -> p a t q", t=TC, a=2)
                        for blk in range(BLOCKS):
                            for a in range(2):
                                m = nc.tensor.matmul(pq2[a * 64:(a + 1) * 64, blk], w_q2[:, blk], by_parity[:, a],
                                                     start=True, stop=True, skip_group_check=True)
                        m.then_inc(q2_in_psum, 1)

            end_phase(nc, sems1)

        c_t = [sb(f"c{n}", [P, KEYS]) for n in range(2)]
        k_hi = sb("k_hi", [P, KEYS + 1], F32R)
        k_lo = sb("k_lo", [P, KEYS], F32R)
        k_block = [sb(f"k_block{n}", [KR, BLOCKS, KEYS], F32R) for n in range(2)]
        q_hi = [sb(f"q_hi{n}", [KR, BLOCKS * BC], F32R) for n in range(2)]
        q_lo = [sb(f"q_lo{n}", [64, BLOCKS * BC], F32R) for n in range(2)]
        q_top = sb("q_top", [P, BLOCKS, S], F32R)
        q_rest = sb("q_rest", [P, BLOCKS, S])
        block_mask = sb("block_mask", [P, H // BLOCKS])
        q_bd_r = [sb(f"q_bd_r{n}", [P, H * S], F32R) for n in range(2)]
        v_t = [sb(f"v{n}", [P, NT, PAIRS, VW]) for n in range(2)]
        part_max = sb("part_max", [P, PAIRS, NC])
        neg_max = sb("neg_max", [P, PAIRS])
        pair_mask = sb("pair_mask", [PAIRS, PAIRS])
        expo = [sb(f"expo{n}", [P, PAIRS * Q]) for n in range(4)]
        sel = sb("sel", [P, P])
        o_sb = sb("o_sb", [P, 2 * Q])
        r_sb = sb("r_sb", [P, 2 * Q])
        o_n = sb("o_n", [P, 2 * Q])
        y = sb("y", [P, P])
        ps_a = st.enter_context(nc.psum_tensor(f"{name}_ps_a", [P, 2, 512], F32))
        ps_b = st.enter_context(nc.psum_tensor(f"{name}_ps_b", [P, 2, 2, 512], F32))
        ps_o = st.enter_context(nc.psum_tensor(f"{name}_ps_o", [P, 512], F32))
        ps_m = st.enter_context(nc.psum_tensor(f"{name}_ps_m", [P, 512], F32))

        wait_carried = sem("wait_carried")
        consts_loaded = sem("consts_loaded")
        zeroed = sem("zeroed")
        c_loaded = [sem(f"c_loaded{n}") for n in range(2)]
        q_first_spread = sem("q_first_spread")
        q_spread = sem("q_spread")
        k_in_psum = sem("k_in_psum")
        k_ready = sem("k_ready")
        v_in_psum = sem("v_in_psum")
        v_ready = sem("v_ready")
        first_in_psum = sem("first_in_psum")
        first_max = sem("first_max")
        max_ready = sem("max_ready")
        max_turned = sem("max_turned")
        k_lo_ready = sem("k_lo_ready")
        k_loaded = [sem(f"k_loaded{n}") for n in range(2)]
        q_top_ready = sem("q_top_ready")
        q_rest_ready = sem("q_rest_ready")
        max_spread = sem("max_spread")
        second_in_psum = sem("second_in_psum")
        exp_ready = sem("exp_ready")
        pv_done = sem("pv_done")
        o_copied = sem("o_copied")
        den_in_psum = sem("den_in_psum")
        rden_ready = sem("rden_ready")
        o_normed = sem("o_normed")
        out_in_psum = sem("out_in_psum")
        out_ready = sem("out_ready")
        stored = [sem(f"stored{n}") for n in range(2)]

        ctx = dr["ctxT"]
        ov = out.rearrange("(b q) d -> b q d", q=S)

        def over_batches(eng, batch, last=None):
            batch(0, 0, prep=True, finish=False)
            batch(1, 1, prep=True, finish=True)
            with eng.Fori(1, B // 2 - 1) as i:
                batch(i * 2, 0, prep=True, finish=True)
                batch(i * 2 + 1, 1, prep=True, finish=True)
            batch(B - 2, 0, prep=True, finish=True)
            batch(B - 1, 1, prep=False, finish=True)

        def late_steps(n):
            at = [k for k, (kind, _) in enumerate(PLAN[n]) if kind == "A"]
            return PLAN[n][at[-1] + 1:] if at else PLAN[n] if n in (0, 11) else []

        def ring(n):
            return n % 3 if n < NT - 1 else 3

        def steps(n, prep, finish, kinds):
            for kind, u in PLAN[n]:
                if kind in kinds and (finish if kind in "DO" else prep):
                    yield kind, u

        with nc.Block() as block:
            @block.sync
            def _(sp):
                sp.dma_start(sel[:], dr["sel"]).then_inc(consts_loaded, 16)
                sp.dma_start(pair_mask[:], dr["pair_mask"]).then_inc(consts_loaded, 16)
                sp.dma_start(block_mask[:], dr["block_mask"]).then_inc(consts_loaded, 16)

                def load(n, par, first=False):
                    if not first:
                        sp.wait_ge(v_in_psum, (n - 1) * len(VG))
                    sp.sem_inc(wait_carried, 1)
                    sp.dma_start(c_t[par][:], ctx[:, n] if first else ctx[:, bass.ds(n, 1)].rearrange("p a k -> p (a k)")).then_inc(c_loaded[par], 16)

                def spread_keys(n, par, half, first=False):
                    if half == 0 and not first:
                        sp.wait_ge(second_in_psum, (n - 1) * NT)
                        sp.sem_inc(wait_carried, 1)
                    sp.wait_ge(k_lo_ready, n * NC + 2 * half + 2)
                    sp.sem_inc(wait_carried, 1)
                    a, w = HALVES[half]
                    for part, src in enumerate((k_hi, k_lo)):
                        for blk in range(BLOCKS):
                            sp.dma_start(k_block[par][part * 32:(part + 1) * 32, blk, a:a + w].bitcast(F32),
                                         src[blk * 32:(blk + 1) * 32, a:a + w].bitcast(F32)).then_inc(k_loaded[par], 16)

                load(0, 0, True)
                load(1, 1, True)
                for half in range(2):
                    spread_keys(0, 0, half, True)

                def store(b, par):
                    sp.wait_ge(out_ready, b + 1)
                    sp.sem_inc(wait_carried, 1)
                    sp.dma_start(ov[b] if isinstance(b, int) else ov[bass.ds(b, 1)].rearrange("a q d -> (a q) d"),
                                 y[par * S:(par + 1) * S]).then_inc(stored[par], 16)

                def batch(b, par, prep, finish):
                    if not (isinstance(b, int) and b >= B - 2):
                        load(b + 2, par)
                    if prep:
                        for half in range(2):
                            spread_keys(b + 1, 1 - par, half, isinstance(b, int) and b == 0)
                    if finish:
                        store(b - 1, 1 - par)

                over_batches(sp, batch)
                store(B - 1, 1)
                for n in range(2):
                    sp.wait_ge(stored[n], 16 * (B // 2))

            @block.gpsimd
            def _(pool):
                for n in range(2):
                    nc.gpsimd.memset(v_t[n][:], 0.0).then_inc(zeroed, 1)
                    pool.wait_ge(zeroed, 2 * n + 1)
                    nc.gpsimd.memset(v_t[n][:, :, :, 16:17], 1.0).then_inc(zeroed, 1)
                nc.gpsimd.memset(k_hi[:, KEYS:KEYS + 1].bitcast(F32), 0.0).then_inc(zeroed, 1)
                for n in range(2):
                    pool.wait_ge(zeroed, 5 + n)
                    nc.gpsimd.memset(k_block[n][MAX_ROW:KR].bitcast(F32), 1.0).then_inc(zeroed, 1)
                pool.wait_ge(zeroed, 7)
                pool.wait_ge(consts_loaded, 48)

                def spread_first(n, par):
                    if not (isinstance(n, int) and n < 2):
                        pool.wait_ge(first_in_psum, (n - 1) * UNITS)
                    qs = q_all[:, n * S:(n + 1) * S] if isinstance(n, int) else q_all[:, bass.ds(n * S, S)]
                    nc.gpsimd.tensor_tensor(q_bd_r[par][:].rearrange("p (h q) -> p h q", h=H),
                                            qs.unsqueeze(1).broadcast_to([P, H, S]),
                                            head_mask[:].unsqueeze(2).broadcast_to([P, H, S]), ALU.mult).then_inc(q_first_spread, 1)

                def spread_q(n, par):
                    half = slice(par * 64, (par + 1) * 64)
                    at = (n - par) * (S // 2)
                    q2 = q_twice[:, :, at:at + S] if isinstance(n, int) else q_twice[:, :, bass.ds(at, S)]
                    if not (isinstance(n, int) and n == 0):
                        pool.wait_ge(q_spread, n)
                        pool.sem_inc(wait_carried, 1)
                    nc.gpsimd.tensor_copy(q_top[:], q2).then_inc(q_top_ready, 1)
                    pool.wait_ge(q_top_ready, n + 1)
                    pool.sem_inc(wait_carried, 1)
                    nc.gpsimd.tensor_tensor(q_rest[:], q2, q_top[:].bitcast(F32), ALU.subtract).then_inc(q_rest_ready, 1)
                    pool.wait_ge(q_rest_ready, n + 1)
                    if not (isinstance(n, int) and n < 2):
                        pool.wait_ge(second_in_psum, (n - 1) * NT)
                    for blk in range(BLOCKS):
                        m = spread_block(q_hi[par], q_top[half, blk].bitcast(F32), half, blk)
                    for blk in range(BLOCKS):
                        m = spread_block(q_lo[par], q_rest[half, blk], half, blk)
                    m.then_inc(q_spread, 1)

                def spread_block(dst, src, half, blk):
                    hb = H // BLOCKS
                    return nc.gpsimd.tensor_tensor(dst[0:64, blk * BC:(blk + 1) * BC].rearrange("p (h q) -> p h q", h=hb),
                                                   src.unsqueeze(1).broadcast_to([64, hb, S]),
                                                   block_mask[half].unsqueeze(2).broadcast_to([64, hb, S]), ALU.mult)

                spread_first(0, 0)
                spread_first(1, 1)
                pool.wait_ge(q_first_spread, 2)
                spread_q(0, 0)

                def batch(b, par, prep, finish):
                    if prep:
                        spread_q(b + 1, 1 - par)
                    if not (isinstance(b, int) and b >= B - 2):
                        pool.wait_ge(q_spread, b + 2)
                        pool.sem_inc(wait_carried, 1)
                        spread_first(b + 2, par)

                over_batches(pool, batch)

            @block.scalar
            def _(act):
                def key_chunk(n, par, c):
                    a, w = CK[c]
                    if c == 0 and not (isinstance(n, int) and n == 0):
                        act.wait_ge(k_loaded[1 - par], (n - 2 + par) * (PER_BATCH // 2) + PER_BATCH)
                    act.wait_ge(k_in_psum, n * NC + c + 1)
                    nc.scalar.activation(k_hi[:, a:a + w], ps_m[:, 0:w], ACT.Identity, bias=col("L1_xattn_bk")).then_inc(k_ready, 1)

                def values(n, par, g):
                    act.wait_ge(v_in_psum, n * len(VG) + g + 1)
                    full = [t for t in VG[g] if t[1] == P]
                    for lo, cnt, rows in ((0, len(full), P), (len(full), len(VG[g]) - len(full), VG[g][-1][1])):
                        if cnt:
                            m = nc.scalar.activation(
                                v_t[par][0:rows, 4 * g + lo:4 * g + lo + cnt, :, 0:16].rearrange("p t j n -> p (t j) n"),
                                ps_m[0:rows, lo * P:(lo + cnt) * P].rearrange("p (t n) -> p t n", n=16), ACT.Copy)
                    m.then_inc(v_ready, 1)

                act.wait_ge(zeroed, 7)
                for c in range(NC):
                    key_chunk(0, 0, c)
                    values(0, 0, c)

                def copy_o(b):
                    act.wait_ge(pv_done, (b + 1) * NT)
                    nc.scalar.activation(o_sb[:], ps_o[:, 0:2 * Q], ACT.Copy).then_inc(o_copied, 1)

                def batch(b, par, prep, finish):
                    def copy_out(n, late):
                        for kind, c in steps(n, prep, finish, "KV"):
                            if ((kind, c) in late_steps(n)) == late:
                                (key_chunk if kind == "K" else values)(b + 1, 1 - par, c)

                    for n, (k0, kn) in enumerate(KT):
                        copy_out(n, False)
                        act.wait_ge(second_in_psum, b * NT + n + 1)
                        act.wait_ge(pv_done, b * NT + n - 2) if not (isinstance(b, int) and b * NT + n - 2 < 1) else None
                        nc.scalar.activation(expo[ring(n)][0:kn], ps_b[0:kn, (par + n) % 2].rearrange("p a n -> p (a n)"),
                                             ACT.Exp).then_inc(exp_ready, 1)
                        if n == 0 and finish:
                            copy_o(b - 1)
                        copy_out(n, True)

                over_batches(act, batch)
                copy_o(B - 1)

            @block.vector
            def _(dve):
                dve.wait_ge(consts_loaded, 48)

                def keys_low(n, par, c):
                    a, w = CK[c]
                    dve.wait_ge(k_ready, n * NC + c + 1)
                    nc.vector.scalar_tensor_tensor(k_lo[:, a:a + w], ps_m[:, 0:w], col("L1_xattn_bk"), k_hi[:, a:a + w].bitcast(F32),
                                                   ALU.add, ALU.subtract).then_inc(k_lo_ready, 1)

                def row_max(n, u):
                    c, j = divmod(u, PAIRS)
                    dve.wait_ge(first_in_psum, n * UNITS + u + 1)
                    nc.vector.tensor_reduce(part_max[:, j, c:c + 1], ps_a[:, u % 2, 0:CK[c][1]], AX.X, ALU.max).then_inc(first_max, 1)

                def maxima(n):
                    dve.wait_ge(first_max, (n + 1) * UNITS)
                    nc.vector.tensor_reduce(neg_max[:], part_max[:], AX.X, ALU.max, negate=True).then_inc(max_ready, 1)

                def spread_max(n, par):
                    dve.wait_ge(max_turned, n + 1)
                    if not (isinstance(n, int) and n < 2):
                        dve.wait_ge(second_in_psum, (n - 1) * NT)
                    nc.vector.tensor_tensor(q_hi[par][MAX_ROW:KR].rearrange("p (j q) -> p j q", j=PAIRS),
                                            ps_m[0:PAIRS, 0:Q].unsqueeze(1).broadcast_to([PAIRS, PAIRS, Q]),
                                            pair_mask[:].unsqueeze(2).broadcast_to([PAIRS, PAIRS, Q]),
                                            ALU.mult).then_inc(max_spread, 1)

                def normalise(b):
                    dve.wait_ge(den_in_psum, b + 1)
                    nc.vector.reciprocal(r_sb[:], ps_m[:, 0:2 * Q]).then_inc(rden_ready, 1)
                    dve.wait_ge(rden_ready, b + 1)
                    nc.vector.tensor_tensor(o_n[:], o_sb[:], r_sb[:], ALU.mult).then_inc(o_normed, 1)

                def finish_out(b, par):
                    dve.wait_ge(out_in_psum, b + 1)
                    if not (isinstance(b, int) and b < 2):
                        dve.wait_ge(stored[par], (b - par) * 8)
                    half = slice(par * S, (par + 1) * S)
                    tile = x_res[half, b // 2] if isinstance(b, int) else x_res[half, bass.ds(tile_of(b, par), 1)].rearrange("p a d -> p (a d)")
                    nc.vector.tensor_tensor(y[half], ps_m[half, 0:P], tile, ALU.add).then_inc(out_ready, 1)

                pair = [None]

                def tile_of(b, par):
                    return pair[0] if par == 0 else pair[0] - 1

                for c in range(NC):
                    keys_low(0, 0, c)
                    for j in range(PAIRS):
                        row_max(0, c * PAIRS + j)
                maxima(0)
                spread_max(0, 0)

                def batch(b, par, prep, finish):
                    for n in range(NT):
                        for kind, u in steps(n, prep, finish, "DKAOM"):
                            if kind == "D":
                                normalise(b - 1)
                            if kind == "K":
                                keys_low(b + 1, 1 - par, u)
                            if kind == "A":
                                row_max(b + 1, u)
                                if u == UNITS - 1:
                                    maxima(b + 1)
                            if kind == "O":
                                finish_out(b - 1, 1 - par)
                            if kind == "M":
                                spread_max(b + 1, 1 - par)

                batch(0, 0, prep=True, finish=False)
                batch(1, 1, prep=True, finish=True)
                with dve.Fori(1, B // 2 - 1) as i:
                    pair[0] = i
                    batch(i * 2, 0, prep=True, finish=True)
                    batch(i * 2 + 1, 1, prep=True, finish=True)
                batch(B - 2, 0, prep=True, finish=True)
                batch(B - 1, 1, prep=False, finish=True)
                normalise(B - 1)
                finish_out(B - 1, 1)

            @block.tensor
            def _(pe):
                pe.wait_ge(zeroed, 7)
                pe.wait_ge(consts_loaded, 48)

                def keys(n, par, c):
                    a, w = CK[c]
                    if c == 0:
                        pe.wait_ge(c_loaded[par], (n - par) * 8 + 16)
                    nc.tensor.matmul(ps_m[:, 0:w], w_kv[:, 0], c_t[par][:, a:a + w], start=True, stop=True).then_inc(k_in_psum, 1)

                def vals(n, par, g):
                    for t, (k0, kn) in enumerate(VG[g]):
                        m = nc.tensor.matmul(ps_m[0:kn, t * P:(t + 1) * P], c_t[par][:, k0:k0 + kn], w_kv[:, 1],
                                             start=True, stop=True, skip_group_check=True)
                    m.then_inc(v_in_psum, 1)

                def first(n, par, u):
                    c, j = divmod(u, PAIRS)
                    a, w = CK[c]
                    if u == 0:
                        pe.wait_ge(q_first_spread, n + 1)
                    if j == 0:
                        pe.wait_ge(k_ready, n * NC + c + 1)
                    if not (isinstance(n, int) and n * UNITS + u < 2):
                        pe.wait_ge(first_max, n * UNITS + u - 1)
                    w += w % 2
                    nc.tensor.matmul(ps_a[:, u % 2, 0:w], q_bd_r[par][:, j * Q:(j + 1) * Q], k_hi[:, a:a + w],
                                     start=True, stop=True).then_inc(first_in_psum, 1)

                def turn_max(n):
                    pe.wait_ge(max_ready, n + 1)
                    nc.tensor.transpose(ps_m[0:PAIRS, 0:P], neg_max[:], ident[:]).then_inc(max_turned, 1)

                def second(b, par, n, blk):
                    k0, kn = KT[n]
                    if n == 0 and blk == 0:
                        pe.wait_ge(q_spread, b + 1)
                        pe.wait_ge(max_spread, b + 1)
                        pe.wait_ge(k_loaded[par], (b - par) * (PER_BATCH // 2) + PER_BATCH)
                    if blk == 0 and not (isinstance(b, int) and b * NT + n < 2):
                        pe.wait_ge(exp_ready, b * NT + n - 1)
                    dst = ps_b[0:kn, (par + n) % 2, blk // 2, blk % 2 * BC:(blk % 2 + 1) * BC]
                    nc.tensor.matmul(dst, k_block[par][:, blk, k0:k0 + kn], q_hi[par][:, blk * BC:(blk + 1) * BC],
                                     start=True, stop=False, skip_group_check=True)
                    m = nc.tensor.matmul(dst, k_block[par][0:64, blk, k0:k0 + kn], q_lo[par][:, blk * BC:(blk + 1) * BC],
                                         start=False, stop=True, skip_group_check=True)
                    if blk == BLOCKS - 1:
                        m.then_inc(second_in_psum, 1)

                def product(b, par, n, js):
                    k0, kn = KT[n]
                    if js[0] == 0:
                        pe.wait_ge(exp_ready, b * NT + n + 1)
                    if n == 0 and js[0] == 0:
                        pe.wait_ge(v_ready, (b + 1) * len(VG))
                        if not (isinstance(b, int) and b == 0):
                            pe.wait_ge(o_copied, b)
                    for j in js:
                        g, s2 = j % 4, j // 4
                        m = nc.tensor.matmul(ps_o[g * VW:(g + 1) * VW, s2 * Q:(s2 + 1) * Q], v_t[par][0:kn, n, j],
                                             expo[ring(n)][0:kn, j * Q:(j + 1) * Q], start=n == 0 and s2 == 0,
                                             stop=n == NT - 1, skip_group_check=True)
                    if j == PAIRS - 1:
                        m.then_inc(pv_done, 1)

                def denominators(b):
                    pe.wait_ge(o_copied, b + 1)
                    nc.tensor.matmul(ps_m[:, 0:2 * Q], sel[:], o_sb[:], start=True, stop=True).then_inc(den_in_psum, 1)

                def project(b, par):
                    pe.wait_ge(o_normed, b + 1)
                    for k in range(4):
                        m = nc.tensor.matmul(ps_m[par * S:(par + 1) * S, 0:P], o_n[:, k * S:(k + 1) * S], w_o[:, k // 2, k % 2],
                                             start=k == 0, stop=k == 3, skip_group_check=True)
                    m.then_inc(out_in_psum, 1)

                def after(kind, b, u):
                    if kind == "K":
                        pe.wait_ge(k_lo_ready, b * NC + u + 1)
                    if kind == "V":
                        pe.wait_ge(v_ready, b * len(VG) + u + 1)
                    if kind == "M":
                        pe.wait_ge(max_spread, b + 1)
                    if kind == "D":
                        pe.wait_ge(rden_ready, b + 1)
                    if kind == "O":
                        pe.wait_ge(out_ready, b + 1)

                for c in range(NC):
                    if c:
                        after("V", 0, c - 1)
                    keys(0, 0, c)
                    after("K", 0, c)
                    vals(0, 0, c)
                    for j in range(PAIRS):
                        first(0, 0, c * PAIRS + j)
                after("V", 0, NC - 1)
                turn_max(0)

                ORDER = [s for slot in PLAN for s in slot if s[0] != "A"]

                def batch(b, par, prep, finish):
                    users = [s for s in ORDER if (finish if s[0] in "DO" else prep)]

                    def step(kind, u):
                        if kind == "A":
                            first(b + 1, 1 - par, u)
                            return
                        at = users.index((kind, u))
                        if at:
                            prior, pu = users[at - 1]
                            after(prior, b - 1 if prior in "DO" else b + 1, pu)
                        else:
                            after("M", b, 0)
                        if kind == "K":
                            keys(b + 1, 1 - par, u)
                        if kind == "V":
                            vals(b + 1, 1 - par, u)
                        if kind == "D":
                            denominators(b - 1)
                        if kind == "O":
                            project(b - 1, 1 - par)
                        if kind == "M":
                            turn_max(b + 1)

                    for n in range(NT):
                        turns = [x for x in steps(n, prep, finish, "KVDOM")]
                        ups = [x for x in steps(n, prep, finish, "A")]
                        for s in turns:
                            if s not in late_steps(n):
                                step(*s)
                        for k in range(BLOCKS):
                            second(b, par, n, k)
                            if ups and k == (3 if PLAN[n][0][0] == "K" else 1):
                                step(*ups.pop(0))
                        if len(ups) > 2:
                            step(*ups.pop(0))
                        for js in (range(0, 4), range(4, PAIRS)):
                            if n:
                                product(b, par, n - 1, js)
                            elif finish:
                                product(b - 1, 1 - par, NT - 1, js)
                            if ups:
                                step(*ups.pop(0))
                        for s in turns:
                            if s in late_steps(n):
                                step(*s)

                over_batches(pe, batch)
                product(B - 1, 1, NT - 1, range(PAIRS))
                after("O", B - 2, 0)
                denominators(B - 1)
                project(B - 1, 1)
        end_phase(nc, sems)


def build(nc, dr, out):
    def scratch(n):
        return nc.dram_tensor(n, (T, D), F32, kind="Internal").ap()

    x1, x2, x3, x4, x5 = (scratch(f"x_after_{n}") for n in range(1, 6))
    mid0, base0, mid1, base1 = (scratch(n) for n in ("ffn0_mid", "ffn0_base", "ffn1_mid", "ffn1_base"))

    attention_phase(nc, dr, "xattn0", x_in=dr["x0"], outs=[x1], w="w_p1", ctx=dr["ctxT"])
    state_space_phase(nc, dr, "ssm0", x_in=x1, out=x2)
    attention_phase(nc, dr, "ffn0a", x_in=x2, outs=[mid0, base0], w="w_p3", L=B, by_position=True, second_norm="ln",
                    gamma="L0_ffn_ln1_w", beta="L0_ffn_ln1_b", q_bias="L0_ffn_bq", k_bias="L0_ffn_bk",
                    v_bias="L0_ffn_bv", o_bias="L0_ffn_out_proj_b", keep_norm=True)
    moe_phase(nc, dr, "ffn0m", x_in=mid0, base_in=base0, out=x3, E=8, w1="moe0_w1", w2="moe0_w2", router="moe0_rt",
              norm="ln", gamma="L0_ffn_ln2_w", beta="L0_ffn_ln2_b", act_func=ACT.Gelu, top=2, by_position=True)
    cross_attention_phase(nc, dr, "xattn1", x_in=x3, out=x4)
    attention_phase(nc, dr, "attn1", x_in=x4, outs=[x5], w="w_p5", rope=True, alibi=True, o_bias="L1_attn_proj_b")
    attention_phase(nc, dr, "ffn1a", x_in=x5, outs=[mid1, base1], w="w_p6", second_norm="rms", gamma="L1_ffn_norm1_w",
                    rope=True, latent=True, keep_norm=True)
    moe_phase(nc, dr, "ffn1m", x_in=mid1, base_in=base1, out=out, E=4, w1="moe1_w1", w2="moe1_w2", router="moe1_rt",
              norm="rms", gamma="L1_ffn_norm2_w", act_func=ACT.Relu, top=1, b1="moe1_b1", b2="moe1_b2", gate_b="moe1_gb")


def consts():
    c = {}
    c["ident"] = np.eye(P, dtype=np.float32)
    c["head_mask"] = np.repeat(np.eye(H, dtype=np.float32), HD, 0)
    for L in (64, 32):
        q, k = np.arange(P)[:, None] % L, np.arange(L)[None, :]
        m = np.where(q >= k, 0.0, -1e30).astype(np.float32)
        c[f"mask{L}"] = np.ascontiguousarray(np.tile(m, (1, H)).view(np.uint16)[:, 1::2]).view(np.float32)
        hg = P // L
        c[f"v_mask{L}"] = (np.arange(P)[:, None] // L == np.arange(hg * HD)[None, :] // HD).astype(np.float32)
    pos, d = np.arange(P) % S, np.arange(P) % HD
    inv = 1.0 / 10000.0 ** (np.arange(0, HD, 2, dtype=np.float32) / np.float32(HD))
    ang = (pos[None, :].astype(np.float32) * inv.astype(np.float32)[d % 4][:, None]).astype(np.float32)
    cos, sin = np.cos(ang), np.sin(ang) * np.where(d < 4, -1.0, 1.0)[:, None]
    sc = np.float32(HD ** -0.5)
    c["rope"] = np.stack([cos * sc, sin * sc, cos, sin], 1).astype(np.float32)
    q, k = np.arange(P)[:, None] % S, np.arange(S)[None, :]
    c["dist"] = (np.minimum(k - q, 0) * 8.0).astype(np.float32)
    return c


def layout(inputs):
    f = {k: np.asarray(v) for k, v in inputs.items()}
    c = consts()
    rot = np.arange(128) // 8 * 8 + (np.arange(128) % 8 + 4) % 8
    a = dict(c)
    a["x0"] = f["x"].reshape(2048, 128)
    a["ctxT"] = np.ascontiguousarray(f["ctx_1024"].transpose(2, 0, 1))
    st = lambda *w: np.ascontiguousarray(np.stack([x.T for x in w], 1))
    a["w_p1"] = st(f["L0_xattn_Wq"], f["L0_xattn_Wk"], f["L0_xattn_Wv"], f["L0_xattn_Wo"])
    q, k, v = np.split(f["L0_ffn_in_proj_w"], 3)
    a["w_p3"] = st(q, k, v, f["L0_ffn_out_proj_w"])
    q, k, v = np.split(f["L1_attn_qkv_w"], 3)
    a["w_p5"] = st(q, k, q[rot], k[rot], v, f["L1_attn_proj_w"])
    a["w_p6"] = st(f["L1_ffn_Wq"], f["L1_ffn_Wq"], f["L1_ffn_Wq"][rot], f["L1_ffn_Wq"], f["L1_ffn_Wq"], f["L1_ffn_Wo"])
    a["w_lat"] = np.ascontiguousarray(f["L1_ffn_Wdkv"].T)
    a["wk_lat"] = st(f["L1_ffn_Wuk"], f["L1_ffn_Wuk"][rot], f["L1_ffn_Wuv"])
    bq, bk, bv = np.split(f["L0_ffn_in_proj_b"], 3)
    pad = lambda v: np.concatenate([v, np.zeros(128 - v.size, np.float32)])
    cols = [f["L0_attn_ln_gamma"], f["L0_attn_ln_beta"], f["L0_ffn_ln1_w"], f["L0_ffn_ln1_b"], f["L0_ffn_ln2_w"], f["L0_ffn_ln2_b"],
            bq, bk, f["L1_xattn_bq"], f["L1_xattn_bk"], f["L1_ffn_norm1_w"], f["L1_ffn_norm2_w"],
            pad(f["L1_ffn_ln_g"]), pad(f["L1_ffn_ln_b"]), f["L0_attn_conv_b"][:128], f["L0_attn_conv_b"][128:], f["L1_xattn_bv"]]
    a["cols"] = np.ascontiguousarray(np.stack(cols, 1))
    a["rows"] = np.stack([bv, f["L0_ffn_out_proj_b"], f["L1_xattn_bv"], f["L1_xattn_bo"], f["L1_attn_proj_b"]])[None]
    a["slopes"] = np.ascontiguousarray(np.broadcast_to(f["L1_attn_slopes"], (128, 16)))
    blk = lambda w: np.ascontiguousarray(w.reshape(128, 16, 128))
    a["moe0_w1"] = blk(f["L0_ffn_w1"].transpose(1, 0, 2))
    a["moe0_w2"] = np.ascontiguousarray(f["L0_ffn_w2"].reshape(16, 128, 128).transpose(1, 0, 2))
    a["moe0_rt"] = np.ascontiguousarray(f["L0_ffn_router_w"].T)
    a["moe1_w1"] = blk(f["L1_ffn_W1"].transpose(2, 0, 1))
    a["moe1_w2"] = np.ascontiguousarray(f["L1_ffn_W2"].transpose(0, 2, 1).reshape(16, 128, 128).transpose(1, 0, 2))
    a["moe1_rt"] = np.ascontiguousarray(f["L1_ffn_gate_w"].T)
    a["moe1_b1"] = np.ascontiguousarray(f["L1_ffn_b1"].reshape(16, 128).T)
    a["moe1_b2"] = f["L1_ffn_b2"].reshape(1, 512)
    a["moe1_gb"] = f["L1_ffn_gate_b"].reshape(1, 4)
    a["iota"] = np.broadcast_to(np.arange(8, dtype=np.float32), (128, 8)).copy()
    a["ssm_w_in"] = np.ascontiguousarray(f["L0_attn_W_in"].T.reshape(128, 4, 128))
    a["ssm_w_out"] = np.ascontiguousarray(f["L0_attn_W_out"].T.reshape(2, 128, 128).transpose(1, 0, 2))
    wb = np.zeros((128, 2, 32), np.float32); wb[:, :, :16] = f["L0_attn_Bm"].T.reshape(2, 128, 16).transpose(1, 0, 2)
    wc = np.zeros((128, 4, 2, 128), np.float32)
    am, at = np.zeros((128, 128), np.float32), np.zeros((128, 128), np.float32)
    for j in range(4):
        wc[32 * j:32 * j + 16, j] = f["L0_attn_Cm"].reshape(16, 2, 128)
        am[32 * j:32 * j + 16, 32 * j:32 * j + 16] = f["L0_attn_A"]
        at[32 * j:32 * j + 16, 32 * j:32 * j + 16] = f["L0_attn_A"].T
    a["ssm_b"], a["ssm_c"], a["ssm_a"], a["ssm_at"] = wb, wc, am, at
    a["ssm_taps"] = np.ascontiguousarray(f["L0_attn_conv_w"].reshape(2, 128, 4).transpose(1, 0, 2))
    a["w_q4"] = np.ascontiguousarray(f["L1_xattn_Wq"].T)
    wq = a["w_q4"].reshape(128, 4, 32)
    a["w_q4_twice"] = np.ascontiguousarray(np.concatenate([wq, wq], 2))
    a["bq4_twice"] = np.ascontiguousarray(np.tile(f["L1_xattn_bq"].reshape(4, 32).T, (4, 1)))
    a["block_mask"] = np.ascontiguousarray(np.tile(np.repeat(np.eye(4, dtype=np.float32), 8, 0), (4, 1)))
    a["w_o4"] = np.ascontiguousarray(f["L1_xattn_Wo"].T)
    a["w_kv4"] = st(f["L1_xattn_Wk"], f["L1_xattn_Wv"])
    wo = f["L1_xattn_Wo"].T.reshape(2, 4, 2, 8, 128)
    wp = np.zeros((4, 32, 2, 2, 128), np.float32)
    for ab in range(2): wp[:, 8 * ab:8 * ab + 8, :, ab] = wo[:, :, ab].transpose(1, 2, 0, 3)
    a["w_o4_pad"] = wp.reshape(128, 2, 2, 128)
    sel = np.zeros((128, 128), np.float32)
    for g in range(4): sel[32 * g + 16, 32 * g:32 * g + 32] = 1
    a["sel"] = sel
    a["pair_mask"] = np.eye(8, dtype=np.float32)
    return a


def kernel(**inputs):
    from concourse import bacc
    from concourse.bass_utils import run_bass_kernel_spmd

    nc = bacc.Bacc("TRN2", target_bir_lowering=False, num_devices=1)
    arrays = layout(inputs)
    dr = {k: nc.dram_tensor(k, v.shape, mybir.dt.from_np(v.dtype), kind="ExternalInput").ap() for k, v in arrays.items()}
    out = nc.dram_tensor("out", (T, D), F32, kind="ExternalOutput").ap()
    build(nc, dr, out)
    r = run_bass_kernel_spmd(nc, [arrays], core_ids=[0])
    return r.results[0]["out"].reshape(B, S, D)
```
